# Optimizing a Trainium2 kernel written in Bass

```python
import numpy as np
import jax
import jax.numpy as jnp

def _softmax(x, axis=-1):
    return jax.nn.softmax(x, axis=axis)

def _gelu(x):
    return jax.nn.gelu(x, approximate=True)

def _silu(x):
    return jax.nn.silu(x)

def _sigmoid(x):
    return jax.nn.sigmoid(x)

def _layernorm(x, axis=-1, eps=1e-05):
    m = jnp.mean(x, axis=axis, keepdims=True)
    v = jnp.var(x, axis=axis, keepdims=True)
    return (x - m) / jnp.sqrt(v + eps)

def _scatter_add(tgt, idx, src, axis=0):
    return tgt.at[idx].add(src)

def _segment_sum(src, seg, n):
    return jax.ops.segment_sum(src, seg, n)
kernel_name = 'mk_adaln_d1_jaxref_r4_f8030c'

def setup_inputs(seed: int=0):
    np.random.seed(seed)
    _w = jnp.asarray

    def _L0_attn_setup():
        import jax, jax.numpy as jnp
        import numpy as np
        BATCH, SEQ, D_MODEL, D_STATE = (4, 1024, 512, 256)
        key = jax.random.key(seed)
        kx, kb, kc = jax.random.split(key, 3)
        x = jax.random.normal(kx, (BATCH, SEQ, D_MODEL), dtype=jnp.float32)
        B = jax.random.normal(kb, (D_STATE, D_MODEL), dtype=jnp.float32) * 0.01
        C = jax.random.normal(kc, (D_MODEL, D_STATE), dtype=jnp.float32) * 0.01
        D = jnp.zeros((D_MODEL,), dtype=jnp.float32)
        return {'x': x, 'B': B, 'C': C, 'D': D}
    _L0_attn_in = _L0_attn_setup()

    def _L0_ffn_setup():
        import jax, jax.numpy as jnp
        import numpy as np
        E = 8
        K = 2
        DIM = 512
        INTER = 352
        N_SHARED = 2
        STD = 0.02
        key = jax.random.key(seed)
        ks = jax.random.split(key, 9)
        B, S = (2, 512)
        return {'x': jax.random.normal(ks[0], (B, S, DIM), dtype=jnp.float32), 'gate_w': jax.random.normal(ks[1], (E, DIM), dtype=jnp.float32) * STD, 'router_bias': jnp.zeros((E,), dtype=jnp.float32), 'W1': jax.random.normal(ks[2], (E, DIM, INTER), dtype=jnp.float32) * STD, 'W3': jax.random.normal(ks[3], (E, DIM, INTER), dtype=jnp.float32) * STD, 'W2': jax.random.normal(ks[4], (E, INTER, DIM), dtype=jnp.float32) * STD, 'sw1': jax.random.normal(ks[5], (N_SHARED * INTER, DIM), dtype=jnp.float32) * STD, 'sw3': jax.random.normal(ks[6], (N_SHARED * INTER, DIM), dtype=jnp.float32) * STD, 'sw2': jax.random.normal(ks[7], (DIM, N_SHARED * INTER), dtype=jnp.float32) * STD}
    _L0_ffn_in = _L0_ffn_setup()
    _L0_c = _w((lambda *s: np.random.randn(*s).astype(np.float32) * 0.05)(1, 512))
    _L0_wmod = _w((lambda *s: np.random.randn(*s).astype(np.float32) * 0.05)(512, 6 * 512) * 512 ** (-0.5))
    _d = {'L0_attn_x': _L0_attn_in['x'], 'L0_attn_B': _L0_attn_in['B'], 'L0_attn_C': _L0_attn_in['C'], 'L0_attn_D': _L0_attn_in['D'], 'L0_ffn_gate_w': _L0_ffn_in['gate_w'], 'L0_ffn_router_bias': _L0_ffn_in['router_bias'], 'L0_ffn_W1': _L0_ffn_in['W1'], 'L0_ffn_W3': _L0_ffn_in['W3'], 'L0_ffn_W2': _L0_ffn_in['W2'], 'L0_ffn_sw1': _L0_ffn_in['sw1'], 'L0_ffn_sw3': _L0_ffn_in['sw3'], 'L0_ffn_sw2': _L0_ffn_in['sw2'], 'L0_c': _L0_c, 'L0_wmod': _L0_wmod}
    _x0 = _d['L0_attn_x']
    _d['L0_attn_x'] = jax.random.normal(jax.random.fold_in(jax.random.key(seed), 1), (1, 2048, 512), dtype=_x0.dtype)
    del _x0
    return _d

def reference(L0_attn_x, L0_attn_B, L0_attn_C, L0_attn_D, L0_ffn_gate_w, L0_ffn_router_bias, L0_ffn_W1, L0_ffn_W3, L0_ffn_W2, L0_ffn_sw1, L0_ffn_sw3, L0_ffn_sw2, L0_c, L0_wmod):

    def _L0_attn_ref(x, B, C, D):
        import jax, jax.numpy as jnp
        import numpy as np
        BATCH, SEQ, D_MODEL, D_STATE = (4, 1024, 512, 256)
        state = jnp.tanh(jnp.einsum('bsd,nd->bsn', x, B))
        return jnp.einsum('bsn,dn->bsd', state, C) + D * x

    def _L0_ffn_ref(x, gate_w, router_bias, W1, W3, W2, sw1, sw3, sw2):
        import jax, jax.numpy as jnp
        import numpy as np
        E = 8
        K = 2
        DIM = 512
        INTER = 352
        N_SHARED = 2
        STD = 0.02
        B, S, D = x.shape
        X = x.reshape(-1, D)
        T = X.shape[0]
        logits = jnp.einsum('td,ed->te', X, gate_w)
        scores = jax.nn.sigmoid(logits)
        sel = scores + router_bias[None, :]
        _, idx = jax.lax.top_k(sel, K)
        w = jnp.take_along_axis(scores, idx, axis=1)
        w = w / jnp.clip(jnp.sum(w, axis=-1, keepdims=True), 1e-12)
        gate_full = jnp.zeros((T, E), dtype=w.dtype).at[jnp.arange(T)[:, None], idx].set(w)
        h1 = jnp.einsum('td,edh->eth', X, W1)
        h3 = jnp.einsum('td,edh->eth', X, W3)
        y = jnp.einsum('eth,ehd->etd', jax.nn.silu(h1) * h3, W2)
        out = jnp.einsum('etd,te->td', y, gate_full)
        shared = jnp.einsum('th,dh->td', jax.nn.silu(jnp.einsum('td,hd->th', X, sw1)) * jnp.einsum('td,hd->th', X, sw3), sw2)
        out = out + shared
        return out.reshape(B, S, D)
    x = L0_attn_x
    mod = (_silu(L0_c) @ L0_wmod).reshape(L0_c.shape[0], 6, 1, -1)
    sa, ca, ga, sb, cb, gb = (mod[:, 0], mod[:, 1], mod[:, 2], mod[:, 3], mod[:, 4], mod[:, 5])
    ga = (2 * (ga >= 0) - 1) * jnp.maximum(jnp.abs(ga), 0.25)
    gb = (2 * (gb >= 0) - 1) * jnp.maximum(jnp.abs(gb), 0.25)
    h = _layernorm(x, axis=-1) * (1 + ca) + sa
    x = x + ga * _L0_attn_ref(h, L0_attn_B, L0_attn_C, L0_attn_D)
    h = _layernorm(x, axis=-1) * (1 + cb) + sb
    x = x + gb * _L0_ffn_ref(h, L0_ffn_gate_w, L0_ffn_router_bias, L0_ffn_W1, L0_ffn_W3, L0_ffn_W2, L0_ffn_sw1, L0_ffn_sw3, L0_ffn_sw2)
    return x

_drawn_inputs = setup_inputs


def setup_inputs(seed=0):
    import zlib

    import numpy as np

    out = dict(_drawn_inputs(seed))
    spreads = {'L0_attn_D': (0.0, 0.325), 'L0_ffn_router_bias': (0.0, 0.8)}
    factors = {'L0_attn_B': 6.532,
     'L0_attn_C': 6.521,
     'L0_ffn_gate_w': 8.0,
     'L0_ffn_W1': 7.96,
     'L0_ffn_W3': 7.806,
     'L0_ffn_W2': 7.794,
     'L0_ffn_sw1': 3.999,
     'L0_ffn_sw3': 3.911,
     'L0_ffn_sw2': 3.904}
    for name, (base, spread) in spreads.items():
        noise = np.random.default_rng([zlib.crc32(name.encode()), seed]).standard_normal(out[name].shape)
        drawn = base * np.exp(spread * noise) if base else spread * noise
        out[name] = jnp.asarray(drawn.astype(out[name].dtype))
    for name, factor in factors.items():
        out[name] = (out[name] * factor).astype(out[name].dtype)
    return out
```

```python
from contextlib import ExitStack

import concourse.bass as bass
from concourse import mybir

F32 = mybir.dt.float32
F32R = mybir.dt.float32r
BF16 = mybir.dt.bfloat16
I32 = mybir.dt.int32
U32 = mybir.dt.uint32
ALU = mybir.AluOpType
ACT = mybir.ActivationFunctionType
AX = mybir.AxisListType

P = 128
T, D, N, F, E = 2048, 512, 256, 352, 8
KD, KN = D // P, N // P
NT = T // P
NP = NT // 2
KF = -(-F // P)
FP = KF * P
UP = 2 * F
WSZ = KD * UP + KF * D
WDN = KD * UP
SMAX = 2 * T // P + E
SMIN = 2 * T // P
SHARED_A, SHARED_B = E + 1, E
EPS = 1e-5
BIG = 3.0e38

_sizes = [("ident", P), ("tri", P), ("ones", P), ("io", NT * E), ("io8", NT * E),
          ("steps", SMAX), ("thr", NT), ("even", SMAX // 2), ("jseq", E + 2), ("jseq0", E + 2),
          ("par", E + 4)]
COL, _at = {}, 0
for _n, _s in _sizes:
    COL[_n] = (_at, _at + _s)
    _at += _s
CW = _at

TB_OFF, TB_NEED = 0, SMAX
TB_ORDER = 2 * SMAX
TB_FIN = TB_ORDER + E + 2
TB_ZERO = TB_FIN + E + 2
TB_ITERS = TB_ZERO + E + 1
TB_JEND, TB_COFF, TB_CNEED = TB_ITERS + 1, TB_ITERS + 2, TB_ITERS + 3
TB_PAR = TB_ITERS + 4
TBW = TB_PAR + E + 4


def build(nc, x, ccol, wmod, bt, ct, dvec, gwt, rb, w_all, consts, out):
    hs = nc.dram_tensor("hs_rows", (T, D), F32, kind="Internal").ap()
    xs = nc.dram_tensor("xs_rows", (SMAX * P, D), F32, kind="Internal").ap()
    ys = nc.dram_tensor("ys_rows", (SMAX * P, D), F32, kind="Internal").ap()

    with ExitStack() as ctx:
        def sb(name, shape, dt=F32):
            return ctx.enter_context(nc.sbuf_tensor(name, shape, dt))

        def sem(name):
            return ctx.enter_context(nc.semaphore(name))

        bank = [ctx.enter_context(nc.psum_tensor(f"bank{i}", [P, 512], F32)) for i in range(8)]

        cst = sb("cst", [P, CW])

        def const(name):
            return cst[:, COL[name][0]:COL[name][1]]

        ident = const("ident")
        tri_b = sb("tri_b", [P, P], BF16)
        ones_b = sb("ones_b", [P, P], BF16)
        x_all = sb("x_all", [P, NT, D])
        whi = sb("whi", [P, 2 * WSZ], F32R)
        wlo = sb("wlo", [P, 2 * WSZ], F32R)
        raw = sb("raw", [P, WSZ])
        scratch = sb("scratch", [P, 4096])
        mods = sb("mods", [P, 6, D])
        a12 = sb("a12", [P, 2, D])
        bhi = sb("bhi", [P, KD, N], F32R)
        blo = sb("blo", [P, KD, N], F32R)
        chi = sb("chi", [P, KN, D], F32R)
        clo = sb("clo", [P, KN, D], F32R)
        gw = sb("gw", [P, KD, E])
        rbias = sb("rbias", [P, E])
        cols = sb("cols", [P, 2, KD])
        bsa = sb("bsa", [P, KN])
        c_in = sb("c_in", [P, KD])
        sil = sb("sil", [P, KD])
        eps_t = sb("eps_t", [P, 2])
        mhalf = sb("mhalf", [P, 2])
        zrow = sb("zrow", [P, D])
        tbuf = sb("tbuf", [P, 2, D])
        tmpa = sb("tmpa", [P, 2, D])
        h2 = sb("h2", [P, 2, D])
        thi = sb("thi", [P, KD, 2 * P], F32R)
        tlo = sb("tlo", [P, KD, 2 * P], F32R)
        st = sb("st", [P, KN, 2 * P])
        shi = sb("shi", [P, KN, 2 * P], F32R)
        slo = sb("slo", [P, KN, 2 * P], F32R)
        xtf = sb("xtf", [P, 2, D])
        bn1 = sb("bn1", [P, 2, 6])
        bn2 = sb("bn2", [P, 2, 6])
        mv1 = sb("mv1", [P, 2, 2])
        mv2 = sb("mv2", [P, 2, 2])
        ve1 = sb("ve1", [P, 2])
        ve2 = sb("ve2", [P, 2])
        rs1 = sb("rs1", [P, 2])
        rs2 = sb("rs2", [P, 2])
        lg = sb("lg", [P, NT, E])
        sc = sb("sc", [P, NT, E])
        oh = [sb("oh1", [P, NT, E]), sb("oh2", [P, NT, E])]
        rm = sb("rm", [P, NT])
        ri = sb("ri", [P, NT])
        mask = sb("mask", [P, NT, E], BF16)
        msum = sb("msum", [P, E], BF16)
        sw = sb("sw", [P, 2, NT])
        den = sb("den", [P, NT])
        wts = sb("wts", [P, NT, 2])
        pos = sb("pos", [P, NT, 2])
        nE = sb("nE", [P, E])
        idx = [[sb(f"idx{j}{k}", [P, 1], U32) for k in range(2)] for j in range(2)]
        tf = sb("tf", [1, TBW])
        ti = sb("ti", [1, TBW], I32)
        tl = sb("tl", [P, E])
        cum = sb("cum", [P, E])
        base = sb("base", [P, E])
        ne = sb("ne", [1, E])
        alt = sb("alt", [1, E])
        zt = sb("zt", [1, E + 1])
        ordn = sb("ordn", [1, E])
        tq = sb("tq", [1, SMAX + 1])
        tqi = sb("tqi", [1, SMAX + 1], I32)
        xthi = thi[:, :, :].rearrange("p a b -> p (a b)").rearrange("p (b d) -> p b d", b=2)
        xtlo = tlo[:, :, :].rearrange("p a b -> p (a b)").rearrange("p (b d) -> p b d", b=2)
        xin = scratch[:, 0:2 * D].rearrange("p (b d) -> p b d", b=2)
        s1 = scratch[:, 2 * D:2 * D + F]
        gbuf = scratch[:, 3 * D:3 * D + FP]
        ybuf = scratch[:, 4 * D:6 * D].rearrange("p (b d) -> p b d", b=2)
        sel, ra, rc = (scratch[:, 6 * D + n * NT * E:6 * D + (n + 1) * NT * E].rearrange("p (t e) -> p t e", e=E)
                       for n in range(3))
        big3 = scratch[:, 7 * D:7 * D + SMAX * E + 8]
        gth = shi[:, :, :].rearrange("p a b -> p (a b)")
        gtl = slo[:, :, :].rearrange("p a b -> p (a b)")
        btr = raw[:, 0:KD * N].rearrange("p (k n) -> p k n", k=KD)
        ctr = raw[:, 1024:1024 + KN * D].rearrange("p (k n) -> p k n", k=KN)
        cga = raw[:, 2048:2048 + KN * D].rearrange("p (k n) -> p k n", k=KN)
        dbc = raw[:, 3072:3072 + D]
        silb = tmpa[:, 0, :].rearrange("p (k m) -> p k m", k=KD)
        ring = scratch[:, :].rearrange("p (r k n) -> p r k n", r=2, k=KD)

        l_small = sem("l_small")
        l_attn = sem("l_attn")
        l_x = [sem(f"l_x{g}") for g in range(4)]
        l_wm = [sem(f"l_wm{j}") for j in range(2)]
        s_sil = sem("s_sil")
        s_silb = sem("s_silb")
        s_mod = sem("s_mod")
        s_modc = sem("s_modc")
        s_colT = sem("s_colT")
        s_cols = sem("s_cols")
        s_bsaT = sem("s_bsaT")
        s_fold = sem("s_fold")
        s_rawfree = sem("s_rawfree")
        s_cst = sem("s_cst")
        chain = sem("chain")
        pchain = sem("pchain")
        s_bn1, s_st1, s_rs1, s_ve1 = sem("s_bn1"), sem("s_st1"), sem("s_rs1"), sem("s_ve1")
        s_bn2, s_st2, s_rs2, s_ve2 = sem("s_bn2"), sem("s_st2"), sem("s_rs2"), sem("s_ve2")
        s_t = sem("s_t")
        s_tT = sem("s_tT")
        s_thi = sem("s_thi")
        s_tlo = sem("s_tlo")
        s_stp = sem("s_stp")
        s_tanh = sem("s_tanh")
        s_shi = sem("s_shi")
        s_slo = sem("s_slo")
        s_xa, s_xb, s_xd = sem("s_xa"), sem("s_xb"), sem("s_xd")
        s_at = sem("s_at")
        s_x1 = sem("s_x1")
        s_u = sem("s_u")
        s_h2 = sem("s_h2")
        s_nat = sem("s_nat")
        s_h2T = sem("s_h2T")
        s_xtf = sem("s_xtf")
        s_gate = sem("s_gate")
        s_lg = sem("s_lg")
        s_sc = sem("s_sc")
        s_mask = sem("s_mask")
        s_rank = sem("s_rank")
        s_pos = sem("s_pos")
        s_tab = sem("s_tab")
        s_pad = sem("s_pad")
        w_hi, w_raw, w_ready = sem("w_hi"), sem("w_raw"), sem("w_ready")
        q = {}
        for sec in "ABC":
            for n in ("xt", "xhi", "xlo", "up", "silu", "g", "gt", "ghi", "glo", "dn", "y", "idx", "g8"):
                q[sec, n] = sem(f"{n}_{sec}")
            q[sec, "xin"] = [sem(f"xin{j}_{sec}") for j in range(2)]
            q[sec, "ydma"] = [sem(f"ydma{j}_{sec}") for j in range(2)]
        s_scat = [sem(f"s_scat{j}") for j in range(2)]
        s_gath = [sem(f"s_gath{j}") for j in range(2)]
        s_c2, s_c3, s_c4 = sem("s_c2"), sem("s_c3"), sem("s_c4")

        block = ctx.enter_context(nc.Block())
        WM = [1, 0, 2, 4, 3, 5]

        def iterations(eng, body):
            for it in range(3):
                body(it, it, it)
            with eng.Fori(3, NP) as it:
                body(it, 3, NP - 1)
            for it in range(NP, NP + 3):
                body(it, it, it)

        at = [0]

        def value(eng, v):
            if isinstance(v, int):
                return v
            at[0] += 1
            reg = eng.alloc_register(f"value{at[0]}")
            eng.reg_mov(reg, v)
            return reg

        def pairs_of_b(eng):
            return eng.value_load(ti[0:1, TB_ITERS:TB_ITERS + 1], min_val=NP - 2, max_val=SMAX // 2 - 2) + 2

        def live(lag, lo, hi):
            return lo - lag >= 0 and hi - lag < NP

        def steps(eng, count, step):
            for j in range(2):
                step(0, j, j == 0, False)
            with eng.Fori(1, count - 1) as i:
                for j in range(2):
                    step(i, j, False, False)
            for j in range(2):
                step(count - 1, j, False, j == 1)

        @block.sync
        def _(sp):
            wm_v = wmod.rearrange("(k p) (j n) -> j p k n", p=P, j=6)
            x_v = x.rearrange("(g b p) d -> g p b d", b=4, p=P)

            def piece(i):
                if i >= 2:
                    sp.wait_ge(s_mod, i - 1)
                sp.dma_start(ring[:, i % 2, :, :], wm_v[WM[i]]).then_inc(l_wm[i % 2], 16)

            def tiles(g):
                sp.dma_start(x_all[:, 4 * g:4 * g + 4, :], x_v[g]).then_inc(l_x[g], 16)

            sp.dma_start(c_in[:, :], ccol).then_inc(l_small, 16)
            sp.dma_start(cst[:, :], consts).then_inc(l_small, 16)
            sp.dma_start(gw[:, :, :], gwt).then_inc(l_small, 16)
            sp.dma_start(rbias[:, :], rb.to_broadcast([P, E])).then_inc(l_small, 16)
            piece(0)
            piece(1)
            sp.dma_start(btr, bt).then_inc(l_attn, 16)
            sp.dma_start(dbc, dvec.to_broadcast([P, D])).then_inc(l_attn, 16)
            sp.dma_start(ctr, ct).then_inc(l_attn, 16)
            tiles(0)
            for i in range(2, 6):
                piece(i)
            for g in range(1, 4):
                tiles(g)
            sp.wait_ge(pchain, 3)
            sp.dma_start(ys[SMIN * P:, :].rearrange("(s p) d -> p s d", p=P),
                         zrow[:, :].unsqueeze(1).to_broadcast([P, SMAX - SMIN, D])).then_inc(s_pad, 16)
            with sp.Fori(0, NP) as p:
                sp.wait_ge(s_h2, p * 2 + 2)
                sp.dma_start(hs[bass.ds(p * 2 * P, 2 * P), :].rearrange("(b p) d -> p b d", p=P),
                             h2[:, :, :]).then_inc(s_nat, 16)

            def load(sec, j, row):
                src = xs if sec == "B" else hs
                sp.dma_start(xin[:, j, :], src[bass.ds(row, P), :]).then_inc(q[sec, "xin"][j], 16)

            sp.wait_ge(s_nat, 16 * NP)
            sp.wait_ge(s_mod, 6)
            for j in range(2):
                load("A", j, j * P)
            sp.wait_ge(s_tab, 1)
            for e in range(E + 1):
                row = sp.value_load(ti[0:1, TB_ZERO + e:TB_ZERO + e + 1], min_val=0, max_val=(SMAX - 1) * P)
                sp.dma_start(xs[bass.ds(row, P), :], zrow[:, :]).then_inc(s_pad, 16)
            with sp.Fori(0, NP - 1) as i:
                for j in range(2):
                    sp.wait_ge(q["A", "xt"], i * 2 + (j + 1))
                    sp.wait_ge(s_scat[j], i * 32 + 32)
                    load("A", j, i * (2 * P) + (2 * P + j * P))
            for j in range(2):
                sp.wait_ge(s_scat[j], 32 * NP)

            iters = pairs_of_b(sp)
            sp.wait_ge(q["A", "xt"], NT)
            for j in range(2):
                load("B", j, j * P)

            def stream(sec, count, store):
                def part(i, j, first):
                    n, m = i * 2 + j, 1 - j
                    sp.wait_ge(q[sec, "xt"], i * 2 + (j + 2))
                    load(sec, m, i * (2 * P) + (j + 3) * P)
                    if not first:
                        store(i - 1 + j, m)

                sp.wait_ge(q[sec, "xt"], 1)
                load(sec, 0, 2 * P)
                part(0, 0, True)
                part(0, 1, False)
                with sp.Fori(1, count - 2) as i:
                    for j in range(2):
                        part(i, j, False)
                part(count - 2, 0, False)
                store(count - 2, 0)
                store(count - 2, 1)
                for j in range(2):
                    store(count - 1, j)

            def store_y(i, j):
                sp.wait_ge(q["B", "y"], i * 2 + (j + 1))
                sp.dma_start(ys[bass.ds(i * (2 * P) + j * P, P), :], ybuf[:, j, :]).then_inc(q["B", "ydma"][j], 16)

            stream("B", iters, store_y)

            sp.wait_ge(q["B", "xt"], iters * 2)
            for j in range(2):
                load("C", j, j * P)

            def store_out(i, j):
                sp.wait_ge(s_c4, i * 2 + (j + 1))
                sp.dma_start(out[bass.ds(i * (2 * P) + j * P, P), :], ybuf[:, j, :]).then_inc(q["C", "ydma"][j], 16)

            stream("C", NP, store_out)
            for j in range(2):
                sp.wait_ge(q["C", "ydma"][j], 16 * NP)

        @block.gpsimd
        def _(pool):
            pool.memset(eps_t[:, :], EPS).then_inc(pchain, 1)
            pool.memset(mhalf[:, :], -0.5).then_inc(pchain, 1)
            pool.memset(zrow[:, :], 0.0).then_inc(pchain, 1)
            pool.wait_ge(pchain, 3)

            def fetch(row, off, slot_free):
                pool.dma_start(raw[:, :], w_all[bass.ds(row * P, P), :]).then_inc(w_raw, 16)
                slot_free()
                pool.dma_start(whi[:, bass.ds(off, WSZ)], w_all[bass.ds(row * P, P), :],
                               max_dma_last_dim=8192).then_inc(w_hi, 16)

            def low(n, off):
                pool.wait_ge(w_raw, n * 16 + 16)
                pool.wait_ge(w_hi, n * 16 + 16)
                pool.tensor_tensor(wlo[:, bass.ds(off, WSZ)], raw[:, :],
                                   whi[:, bass.ds(off, WSZ)].bitcast(F32), ALU.subtract).then_inc(w_ready, 1)

            def body(it, lo, hi):
                if live(0, lo, hi):
                    pool.wait_ge(s_st1, it * 2 + 2)
                    pool.tensor_tensor(ve1[:, :], mv1[:, :, 1], eps_t[:, :], ALU.add).then_inc(s_ve1, 1)
                    pool.wait_ge(s_ve1, it + 1)
                    if lo > 0:
                        pool.wait_ge(s_t, it * 2)
                    pool.tensor_tensor(rs1[:, :], ve1[:, :], mhalf[:, :], ALU.pow).then_inc(s_rs1, 1)
                if live(2, lo, hi):
                    p = it - 2
                    pool.wait_ge(s_st2, p * 2 + 2)
                    pool.tensor_tensor(ve2[:, :], mv2[:, :, 1], eps_t[:, :], ALU.add).then_inc(s_ve2, 1)
                    pool.wait_ge(s_ve2, p + 1)
                    if lo > 2:
                        pool.wait_ge(s_h2, p * 2)
                    pool.tensor_tensor(rs2[:, :], ve2[:, :], mhalf[:, :], ALU.pow).then_inc(s_rs2, 1)
                if live(1, lo, hi):
                    p = it - 1
                    pool.wait_ge(s_t, p * 2 + 2)
                    for j in range(2):
                        pool.tensor_tensor(tmpa[:, j, :], tbuf[:, j, :], a12[:, 0, :], ALU.mult).then_inc(s_xa, 1)
                    pool.wait_ge(s_xa, p * 2 + 2)
                    for j in range(2):
                        pool.tensor_tensor(tmpa[:, j, :], tmpa[:, j, :], a12[:, 1, :], ALU.add).then_inc(s_xb, 1)
                    pool.wait_ge(s_xb, p * 2 + 2)
                    xp = x_all[:, bass.ds(p * 2, 2), :]
                    pool.tensor_tensor(xp, xp, tmpa[:, :, :], ALU.add).then_inc(s_xd, 1)

            pool.wait_ge(s_fold, 1)
            pool.wait_ge(s_mod, 6)
            fetch(SHARED_A, 0, lambda: None)
            iterations(pool, body)
            low(0, 0)

            def table(at, low_, high_):
                return pool.value_load(ti[0:1, bass.ds(at, 1)], min_val=low_, max_val=high_)

            pool.wait_ge(s_tab, 1)
            pool.wait_ge(w_ready, 1)
            fetch(table(TB_ORDER, 0, E - 1), WSZ, lambda: None)
            pool.wait_ge(s_pad, 16 * (E + 2))
            with pool.Fori(0, NP) as i:
                for j in range(2):
                    landed, known = value(pool, i * 16 + 16), value(pool, i * 4 + (2 * j + 2))
                    pool.wait_ge(s_tab, 1)
                    pool.wait_ge(q["A", "xin"][j], landed)
                    pool.wait_ge(q["A", "idx"], known)
                    for k in range(2):
                        pool.indirect_dma_start(xs[:, :], bass.IndirectOffsetOnAxis(ap=idx[j][k][:, :], axis=0),
                                                xin[:, j, :], None).then_inc(s_scat[j], 16)
            low(1, WSZ)
            jend = table(TB_JEND, 3, E + 2)
            with pool.Fori(2, jend) as n:
                row = table(n + (TB_ORDER - 1), 0, E)
                fin = table(n + (TB_FIN - 2), 0, SMAX)
                off = table(n + (TB_PAR), 0, WSZ)
                pool.wait_ge(w_ready, n)
                fetch(row, off, lambda: (pool.wait_ge(q["A", "dn"], NT), pool.wait_ge(q["B", "dn"], fin)))
                low(n, off)
            iters = pairs_of_b(pool)
            stored = value(pool, iters * 16)
            pool.wait_ge(s_tab, 1)
            for j in range(2):
                pool.wait_ge(q["B", "ydma"][j], stored)

            def gather(i, j, first):
                known, used = value(pool, i * 4 + (2 * j + 2)), None if first else value(pool, i * 2 + (j - 1))
                pool.wait_ge(s_tab, 1)
                pool.wait_ge(q["C", "idx"], known)
                if not first:
                    pool.wait_ge(s_c2, used)
                for k, dst in ((0, tbuf), (1, xtf)):
                    pool.indirect_dma_start(dst[:, j, :], None, ys[:, :],
                                            bass.IndirectOffsetOnAxis(ap=idx[j][k][:, :], axis=0)
                                            ).then_inc(s_gath[j], 16)

            for j in range(2):
                gather(0, j, True)
            with pool.Fori(1, NP) as i:
                for j in range(2):
                    gather(i, j, False)

        @block.scalar
        def _(act):
            def body(it, lo, hi):
                if live(1, lo, hi):
                    p = it - 1
                    act.wait_ge(s_tT, p + 1)
                    if lo > 1:
                        act.wait_ge(s_stp, p)
                    for j in range(2):
                        act.activation(thi[:, :, j * P:j * P + P],
                                       bank[2 + j][:, :].rearrange("p (k m) -> p k m", k=KD),
                                       ACT.Copy).then_inc(s_thi, 1)
                if live(3, lo, hi):
                    p = it - 3
                    act.wait_ge(s_h2T, p + 1)
                    if lo > 3:
                        act.wait_ge(s_gate, p)
                    for j in range(2):
                        act.activation(xtf[:, j, :], bank[4 + j][:, :], ACT.Copy).then_inc(s_xtf, 1)
                if live(1, lo, hi):
                    p = it - 1
                    act.wait_ge(s_stp, p + 1)
                    if lo > 1:
                        act.wait_ge(s_slo, p)
                    for n in range(KN):
                        act.activation(st[:, n, :], bank[6][:, n * 2 * P:(n + 1) * 2 * P], ACT.Tanh,
                                       bias=bsa[:, n:n + 1]).then_inc(s_tanh, 1)
                    act.wait_ge(s_tanh, p * 2 + 2)
                    if lo > 1:
                        act.wait_ge(s_at, p)
                    act.activation(shi[:, :, :], st[:, :, :], ACT.Copy).then_inc(s_shi, 1)
                if live(3, lo, hi):
                    p = it - 3
                    act.wait_ge(s_gate, p + 1)
                    act.activation(lg[:, bass.ds(p * 2, 2), :],
                                   bank[7][:, 0:2 * E].rearrange("p (b e) -> p b e", b=2),
                                   ACT.Copy).then_inc(s_lg, 1)

            act.wait_ge(l_small, 64)
            act.activation(sil[:, :], c_in[:, :], ACT.Silu).then_inc(s_sil, 1)
            act.wait_ge(s_fold, 1)
            iterations(act, body)
            act.wait_ge(s_lg, NP)
            act.activation(sc[:, :, :], lg[:, :, :], ACT.Sigmoid).then_inc(s_sc, 1)

            def high(sec, i, j):
                act.wait_ge(q[sec, "xt"], i * 2 + (j + 1))
                act.activation(xthi[:, j, :], bank[j][:, :], ACT.Copy).then_inc(q[sec, "xhi"], 1)

            def result(i, j, first):
                act.wait_ge(q["B", "dn"], i * 2 + (j + 1))
                if not first:
                    act.wait_ge(q["B", "ydma"][j], i * 16)
                act.activation(ybuf[:, j, :], bank[5 + j][:, :], ACT.Copy).then_inc(q["B", "y"], 1)

            def section(sec):
                def step(i, j, first, last):
                    if not last:
                        if not first:
                            act.wait_ge(q[sec, "up"], i * 2 + j)
                        high(sec, i + j, 1 - j)
                    act.wait_ge(q[sec, "up"], i * 2 + (j + 1))
                    if not first:
                        act.wait_ge(q[sec, "g"], i * 2 + j)
                    act.activation(s1, bank[2][:, 0:F], ACT.Silu).then_inc(q[sec, "silu"], 1)
                    act.wait_ge(q[sec, "gt"], i * 2 + (j + 1))
                    if not first:
                        act.wait_ge(q[sec, "dn"], i * 2 + j)
                    act.activation(gth[:, 0:FP], bank[4][:, 0:FP], ACT.Copy).then_inc(q[sec, "ghi"], 1)
                    if sec == "B" and not first:
                        result(i - 1 + j, 1 - j, isinstance(i, int) and i <= 1 - j)
                return step

            act.wait_ge(s_at, NP)
            act.wait_ge(s_stp, NP)
            high("A", 0, 0)
            steps(act, NP, section("A"))
            act.wait_ge(q["A", "dn"], NT)
            act.wait_ge(q["A", "g"], NT)
            act.wait_ge(s_tab, 1)
            iters = pairs_of_b(act)
            high("B", 0, 0)
            steps(act, iters, section("B"))
            result(iters - 1, 1, False)
            act.wait_ge(q["B", "g"], iters * 2)
            high("C", 0, 0)
            steps(act, NP, section("C"))

        @block.tensor
        def _(pe):
            def product(dst, pairs):
                n = len(pairs)
                for m, (ah, al, bh, bl) in enumerate(pairs):
                    pe.matmul(dst, ah, bh, start=(m == 0), stop=False)
                    pe.matmul(dst, ah, bl, start=False, stop=False)
                    mm = pe.matmul(dst, al, bh, start=False, stop=(m == n - 1))
                return mm

            pe.wait_ge(s_silb, KD)
            for i in range(6):
                pe.wait_ge(l_wm[i % 2], 16 * (i // 2 + 1))
                if i >= 2:
                    pe.wait_ge(s_modc, i - 1)
                for k in range(KD):
                    mm = pe.matmul(bank[i % 2][:, :], silb[:, k, :], ring[:, i % 2, k, :],
                                   start=(k == 0), stop=(k == KD - 1))
                mm.then_inc(s_mod, 1)
                if i == 2:
                    pe.wait_ge(s_modc, 2)
                    for j in range(2):
                        for k in range(KD):
                            mm = pe.transpose(bank[4 + j][:, k * P:(k + 1) * P],
                                              mods[:, j, k * P:(k + 1) * P], ident)
                    mm.then_inc(s_colT, 1)
                    pe.wait_ge(s_cols, 1)
                    pe.wait_ge(l_attn, 48)
                    for n in range(KN):
                        for k in range(KD):
                            mm = pe.matmul(bank[6][:, n:n + 1], btr[:, k, n * P:(n + 1) * P],
                                           cols[:, 0, k:k + 1], start=(k == 0), stop=(k == KD - 1))
                    mm.then_inc(s_bsaT, 1)

            def transposes(dst, src):
                for k in range(KD):
                    mm = pe.transpose(dst[:, k * P:(k + 1) * P], src[:, k * P:(k + 1) * P], ident)
                return mm

            def body(it, lo, hi):
                if live(2, lo, hi):
                    p = it - 2
                    pe.wait_ge(s_slo, p + 1)
                    if lo > 2:
                        pe.wait_ge(s_x1, p * 2)
                    for j in range(2):
                        t = slice(j * P, (j + 1) * P)
                        mm = product(bank[j][:, :], [(shi[:, n, t], slo[:, n, t], chi[:, n, :], clo[:, n, :])
                                                     for n in range(KN)])
                    mm.then_inc(s_at, 1)
                if live(1, lo, hi):
                    p = it - 1
                    pe.wait_ge(s_t, p * 2 + 2)
                    if lo > 1:
                        pe.wait_ge(s_tlo, p * 2)
                    for j in range(2):
                        mm = transposes(bank[2 + j], tbuf[:, j, :])
                    mm.then_inc(s_tT, 1)
                if live(3, lo, hi):
                    p = it - 3
                    pe.wait_ge(s_h2, p * 2 + 2)
                    if lo > 3:
                        pe.wait_ge(s_xtf, p * 2)
                    for j in range(2):
                        mm = transposes(bank[4 + j], h2[:, j, :])
                    mm.then_inc(s_h2T, 1)
                if live(1, lo, hi):
                    p = it - 1
                    pe.wait_ge(s_thi, p * 2 + 2)
                    pe.wait_ge(s_tlo, p * 2 + 2)
                    if lo > 1:
                        pe.wait_ge(s_tanh, p * 2)
                    for n in range(KN):
                        t = slice(n * P, (n + 1) * P)
                        mm = product(bank[6][:, n * 2 * P:(n + 1) * 2 * P],
                                     [(bhi[:, k, t], blo[:, k, t], thi[:, k, :], tlo[:, k, :]) for k in range(KD)])
                    mm.then_inc(s_stp, 1)
                if live(3, lo, hi):
                    p = it - 3
                    pe.wait_ge(s_xtf, p * 2 + 2)
                    if lo > 3:
                        pe.wait_ge(s_lg, p)
                    for j in range(2):
                        for k in range(KD):
                            mm = pe.matmul(bank[7][:, j * E:(j + 1) * E], xtf[:, j, k * P:(k + 1) * P],
                                           gw[:, k, :], start=(k == 0), stop=(k == KD - 1))
                    mm.then_inc(s_gate, 1)

            pe.wait_ge(s_modc, 6)
            pe.wait_ge(s_fold, 1)
            iterations(pe, body)

            pe.wait_ge(s_mask, 1)
            pe.wait_ge(s_lg, NP)
            pe.matmul(bank[7][:, 0:NT * E], tri_b[:, :], mask[:, :, :], start=True, stop=False)
            for m in range(NT - 1):
                pe.matmul(bank[7][:, (m + 1) * E:NT * E], ones_b[:, :],
                          mask[:, m:m + 1, :].to_broadcast([P, NT - 1 - m, E]),
                          start=False, stop=(m == NT - 2))
            pe.matmul(bank[7][:, NT * E:(NT + 1) * E], ones_b[:, :], msum[:, :],
                      start=True, stop=True).then_inc(s_rank, 1)

            def turn(sec, i, j):
                pe.wait_ge(q[sec, "xin"][j], i * 16 + 16)
                transposes(bank[j], xin[:, j, :]).then_inc(q[sec, "xt"], 1)

            def up(sec, i, j, off):
                pe.wait_ge(q[sec, "xlo"], i * 2 + (j + 1))
                for m in range(KD):
                    a = slice(m * P, (m + 1) * P)
                    for h in range(2):
                        w = off + (m * UP + h * F)
                        wh, wl = whi[:, bass.ds(w, F)], wlo[:, bass.ds(w, F)]
                        dst = bank[2 + h][:, 0:F]
                        pe.matmul(dst, xthi[:, j, a], wh, start=(m == 0), stop=False)
                        pe.matmul(dst, xthi[:, j, a], wl, start=False, stop=False)
                        mm = pe.matmul(dst, xtlo[:, j, a], wh, start=False, stop=(m == KD - 1))
                mm.then_inc(q[sec, "up"], 1)

            def down(sec, i, j, off, bank_used):
                pe.wait_ge(q[sec, "glo"], i * 2 + (j + 1))
                if bank_used:
                    pe.wait_ge(q[sec, "y"], i * 2 + (j - 1))
                for m in range(KF):
                    a = slice(m * P, (m + 1) * P)
                    w = off + (WDN + m * D)
                    wh, wl = whi[:, bass.ds(w, D)], wlo[:, bass.ds(w, D)]
                    dst = bank[5 + j][:, :]
                    pe.matmul(dst, gth[:, a], wh, start=(m == 0), stop=False)
                    pe.matmul(dst, gth[:, a], wl, start=False, stop=False)
                    mm = pe.matmul(dst, gtl[:, a], wh, start=False, stop=(m == KF - 1))
                mm.then_inc(q[sec, "dn"], 1)

            def section(sec, off_of, look_up=None):
                def step(i, j, first, last):
                    off = off_of(j)
                    if not last:
                        if not first:
                            pe.wait_ge(q[sec, "xlo"], i * 2 + j)
                        turn(sec, i + j, 1 - j)
                    if not first:
                        pe.wait_ge(q[sec, "g"], i * 2 + j)
                    if look_up:
                        pe.wait_ge(w_ready, need)
                    up(sec, i, j, off)
                    if not first:
                        down(sec, i - 1 + j, 1 - j, off_of(1 - j), not (isinstance(i, int) and i <= 1))
                    if look_up and not last:
                        look_up(i * 2 + (j + 1), 1 - j)
                    pe.wait_ge(q[sec, "g"], i * 2 + (j + 1))
                    for m in range(KF):
                        mm = pe.transpose(bank[4][:, m * P:(m + 1) * P], gbuf[:, m * P:(m + 1) * P], ident)
                    mm.then_inc(q[sec, "gt"], 1)
                return step

            pe.wait_ge(s_x1, NT)
            pe.wait_ge(s_tlo, NT)
            pe.wait_ge(s_xtf, NT)
            pe.wait_ge(s_tanh, NT)
            pe.wait_ge(w_ready, 1)
            turn("A", 0, 0)
            steps(pe, NP, section("A", lambda j: 0))
            down("A", NP - 1, 1, 0, True)

            off_b = [pe.alloc_register(f"off_b{j}") for j in range(2)]
            need = pe.alloc_register("need")

            def look_up(n, j):
                pe.reg_mov(off_b[j], pe.value_load(ti[0:1, bass.ds(n + TB_OFF, 1)], min_val=0, max_val=WSZ))
                pe.reg_mov(need, pe.value_load(ti[0:1, bass.ds(n + TB_NEED, 1)], min_val=2, max_val=E + 2))

            pe.wait_ge(s_tab, 1)
            iters = pairs_of_b(pe)
            pe.wait_ge(q["A", "y"], NT)
            turn("B", 0, 0)
            look_up(0, 0)
            def looked_up(j):
                return pe.snap(off_b[j], min_val=0, max_val=WSZ)

            steps(pe, iters, section("B", looked_up, look_up))
            down("B", iters - 1, 1, looked_up(1), True)

            off_c = pe.value_load(ti[0:1, TB_COFF:TB_COFF + 1], min_val=0, max_val=WSZ)
            need_c = pe.value_load(ti[0:1, TB_CNEED:TB_CNEED + 1], min_val=2, max_val=E + 2)
            pe.wait_ge(w_ready, need_c)
            pe.wait_ge(q["B", "y"], iters * 2)
            turn("C", 0, 0)
            steps(pe, NP, section("C", lambda j: off_c))
            down("C", NP - 1, 1, off_c, True)

        @block.vector
        def _(dve):
            count = [0]

            def link(ins):
                count[0] += 1
                ins.then_inc(chain, 1)
                dve.wait_ge(chain, count[0])

            dve.wait_ge(l_small, 64)
            link(dve.tensor_copy(tri_b[:, :], const("tri")))
            link(dve.tensor_copy(ones_b[:, :], const("ones")))
            dve.wait_ge(s_sil, 1)
            for k in range(KD):
                dve.tensor_scalar(silb[:, k, :], const("ones"), sil[:, k:k + 1], None, ALU.mult).then_inc(s_silb, 1)

            t1, t2 = h2[:, 0, :], h2[:, 1, :]
            for i, m in enumerate(WM):
                dve.wait_ge(s_mod, i + 1)
                src, dst = bank[i % 2][:, :], mods[:, m, :]
                if m in (1, 4):
                    dve.tensor_scalar(dst, src, 1.0, None, ALU.add).then_inc(s_modc, 1)
                else:
                    dve.tensor_copy(dst, src).then_inc(s_modc, 1)
                if m in (2, 5):
                    dve.wait_ge(s_modc, i + 1)
                    link(dve.tensor_scalar(t1, dst, 0.0, 2.0, ALU.is_ge, ALU.mult))
                    link(dve.scalar_tensor_tensor(t2, dst, -1.0, dst, ALU.mult, ALU.max))
                    link(dve.tensor_scalar(t2, t2, 0.25, None, ALU.max))
                    link(dve.scalar_tensor_tensor(dst, t1, -1.0, t2, ALU.add, ALU.mult))
                if i == 2:
                    dve.wait_ge(s_modc, 3)
                    dve.wait_ge(s_colT, 1)
                    for j in range(2):
                        cv = bank[4 + j][:, :].rearrange("p (k m) -> p k m", k=KD)[:, :, 0]
                        link(dve.tensor_copy(cols[:, j, :], cv))
                    dve.tensor_copy(t2[:, 0:KD], cols[:, 0, :]).then_inc(s_cols, 1)
                    dve.wait_ge(l_attn, 48)
                    for k in range(KD):
                        link(dve.tensor_scalar(bhi[:, k, :], btr[:, k, :], cols[:, 1, k:k + 1], None, ALU.mult))
                        link(dve.scalar_tensor_tensor(blo[:, k, :], btr[:, k, :], cols[:, 1, k:k + 1],
                                                      bhi[:, k, :].bitcast(F32), ALU.mult, ALU.subtract))
                    for n in range(KN):
                        link(dve.tensor_tensor(cga[:, n, :], ctr[:, n, :], mods[:, 2, :], ALU.mult))
                    link(dve.tensor_copy(chi[:, :, :], cga))
                    link(dve.tensor_tensor(clo[:, :, :], cga, chi[:, :, :].bitcast(F32), ALU.subtract))
                    link(dve.tensor_tensor(a12[:, 0, :], dbc, mods[:, 2, :], ALU.mult))
                    link(dve.tensor_tensor(a12[:, 1, :], a12[:, 0, :], mods[:, 0, :], ALU.mult))
                    link(dve.tensor_tensor(a12[:, 0, :], a12[:, 0, :], mods[:, 1, :], ALU.mult))
                    dve.wait_ge(s_bsaT, 1)
                    dve.tensor_copy(bsa[:, :], bank[6][:, 0:KN]).then_inc(s_fold, 1)
            link(dve.memset(gbuf[:, F:FP], 0.0))

            def body(it, lo, hi):
                if live(2, lo, hi):
                    p = it - 2
                    dve.wait_ge(s_at, p + 1)
                    dve.wait_ge(s_xd, p + 1)
                    for j in range(2):
                        xt = x_all[:, bass.ds(p * 2 + j, 1), :].rearrange("p a d -> p (a d)")
                        dve.tensor_tensor(xt, bank[j][:, :], xt, ALU.add).then_inc(s_x1, 1)
                if live(0, lo, hi):
                    if lo < 3:
                        dve.wait_ge(l_x[lo // 2], 16)
                    for j in range(2):
                        xt = x_all[:, bass.ds(it * 2 + j, 1), :].rearrange("p a d -> p (a d)")
                        dve.bn_stats(bn1[:, j, :], xt).then_inc(s_bn1, 1)
                if live(2, lo, hi):
                    p = it - 2
                    done = value(dve, p * 2 + 2)
                    dve.wait_ge(s_fold, 1)
                    dve.wait_ge(s_x1, done)
                    for j in range(2):
                        xt = x_all[:, bass.ds(p * 2 + j, 1), :].rearrange("p a d -> p (a d)")
                        dve.bn_stats(bn2[:, j, :], xt).then_inc(s_bn2, 1)
                if live(0, lo, hi):
                    done = value(dve, it * 2 + 2)
                    dve.wait_ge(s_fold, 1)
                    dve.wait_ge(s_bn1, done)
                    for j in range(2):
                        dve.bn_aggr(mv1[:, j, :], bn1[:, j, :]).then_inc(s_st1, 1)
                if live(2, lo, hi):
                    done = value(dve, (it - 2) * 2 + 2)
                    dve.wait_ge(s_fold, 1)
                    dve.wait_ge(s_bn2, done)
                    for j in range(2):
                        dve.bn_aggr(mv2[:, j, :], bn2[:, j, :]).then_inc(s_st2, 1)
                if live(1, lo, hi):
                    p = it - 1
                    dve.wait_ge(s_thi, p * 2 + 2)
                    if lo > 1:
                        dve.wait_ge(s_stp, p)
                    for j in range(2):
                        t = slice(j * P, (j + 1) * P)
                        dve.tensor_tensor(tlo[:, :, t], bank[2 + j][:, :].rearrange("p (k m) -> p k m", k=KD),
                                          thi[:, :, t].bitcast(F32), ALU.subtract).then_inc(s_tlo, 1)
                if live(2, lo, hi):
                    p = it - 2
                    dve.wait_ge(s_rs2, p + 1)
                    if lo > 2:
                        dve.wait_ge(s_h2T, p)
                        dve.wait_ge(s_nat, p * 16)
                    for j in range(2):
                        xt = x_all[:, bass.ds(p * 2 + j, 1), :].rearrange("p a d -> p (a d)")
                        dve.scalar_tensor_tensor(h2[:, j, :], xt, mv2[:, j, 0:1], mods[:, 4, :],
                                                 ALU.subtract, ALU.mult).then_inc(s_u, 1)
                    dve.wait_ge(s_u, p * 2 + 2)
                    for j in range(2):
                        dve.scalar_tensor_tensor(h2[:, j, :], h2[:, j, :], rs2[:, j:j + 1], mods[:, 3, :],
                                                 ALU.mult, ALU.add).then_inc(s_h2, 1)
                if live(1, lo, hi):
                    p = it - 1
                    dve.wait_ge(s_shi, p + 1)
                    dve.tensor_tensor(slo[:, :, :], st[:, :, :], shi[:, :, :].bitcast(F32),
                                      ALU.subtract).then_inc(s_slo, 1)
                if live(0, lo, hi):
                    dve.wait_ge(s_rs1, it + 1)
                    if lo > 0:
                        dve.wait_ge(s_tT, it)
                        dve.wait_ge(s_xa, it * 2)
                    for j in range(2):
                        xt = x_all[:, bass.ds(it * 2 + j, 1), :].rearrange("p a d -> p (a d)")
                        dve.tensor_scalar(tbuf[:, j, :], xt, mv1[:, j, 0:1], rs1[:, j:j + 1],
                                          ALU.subtract, ALU.mult).then_inc(s_t, 1)

            for it in range(3):
                body(it, it, it)
            for g in range(1, 4):
                dve.wait_ge(l_x[g], 16)
            with dve.Fori(3, NP) as it:
                body(it, 3, NP - 1)
            for it in range(NP, NP + 3):
                body(it, it, it)

            def tiles_of(t):
                return t[:, :].unsqueeze(2).to_broadcast([P, NT, E])

            io, io8 = (const(n).rearrange("p (t e) -> p t e", e=E) for n in ("io", "io8"))
            dve.wait_ge(s_sc, 1)
            link(dve.tensor_tensor(sel[:, :, :], sc[:, :, :], rbias[:, :].unsqueeze(1).to_broadcast([P, NT, E]),
                                   ALU.add))
            for k in range(2):
                link(dve.tensor_reduce(rm[:, :], sel[:, :, :], AX.X, ALU.max))
                link(dve.tensor_tensor(ra[:, :, :], sel[:, :, :], tiles_of(rm), ALU.is_equal))
                link(dve.scalar_tensor_tensor(rc[:, :, :], ra[:, :, :], -float(E), io8, ALU.mult, ALU.add))
                link(dve.tensor_reduce(ri[:, :], rc[:, :, :], AX.X, ALU.min))
                link(dve.tensor_tensor(oh[k][:, :, :], io, tiles_of(ri), ALU.is_equal))
                link(dve.tensor_tensor(ra[:, :, :], oh[k][:, :, :], sc[:, :, :], ALU.mult))
                link(dve.tensor_reduce(sw[:, k, :], ra[:, :, :], AX.X, ALU.add))
                if k == 0:
                    link(dve.scalar_tensor_tensor(sel[:, :, :], oh[0][:, :, :], -BIG, sel[:, :, :],
                                                  ALU.mult, ALU.add))
            link(dve.tensor_tensor(mask[:, :, :], oh[0][:, :, :], oh[1][:, :, :], ALU.add))
            with nc.allow_low_precision("counts of at most 16 are exact in bfloat16"):
                dve.tensor_reduce(msum[:, :], mask[:, :, :].rearrange("p t e -> p e t"), AX.X,
                                  ALU.add).then_inc(s_mask, 1)
            link(dve.tensor_tensor(den[:, :], sw[:, 0, :], sw[:, 1, :], ALU.add))
            link(dve.tensor_scalar(den[:, :], den[:, :], 1e-12, None, ALU.max))
            link(dve.reciprocal(den[:, :], den[:, :]))
            for k in range(2):
                link(dve.tensor_tensor(wts[:, :, k], sw[:, k, :], den[:, :], ALU.mult))
            dve.wait_ge(s_rank, 1)
            link(dve.tensor_copy(nE[:, :], bank[7][:, NT * E:(NT + 1) * E]))
            b3 = big3[:, 0:E * NT].rearrange("p (e t) -> p e t", e=E)
            link(dve.tensor_tensor(b3, nE[:, :].unsqueeze(2).to_broadcast([P, E, NT]),
                                   const("thr").unsqueeze(1).to_broadcast([P, E, NT]), ALU.is_gt))
            link(dve.tensor_reduce(tl[:, :], b3, AX.X, ALU.add))
            link(dve.tensor_tensor_scan(cum[:, :], const("ones")[:, 0:E], tl[:, :], 0.0, ALU.mult, ALU.add))
            link(dve.tensor_tensor(base[:, :], cum[:, :], tl[:, :], ALU.subtract))
            link(dve.tensor_scalar(base[:, :], base[:, :], float(P), None, ALU.mult))
            link(dve.tensor_tensor(rc[:, :, :], bank[7][:, 0:NT * E].rearrange("p (t e) -> p t e", e=E),
                                   base[:, :].unsqueeze(1).to_broadcast([P, NT, E]), ALU.add))
            for k in range(2):
                link(dve.tensor_tensor(ra[:, :, :], rc[:, :, :], oh[k][:, :, :], ALU.mult))
                link(dve.tensor_reduce(pos[:, :, k], ra[:, :, :], AX.X, ALU.add))

            r0 = slice(0, 1)
            S, J = SMAX, E + 2
            one = const("ones")[r0, 0:E]
            tl0, cum0 = tl[r0, :], cum[r0, :]
            link(dve.tensor_scalar(ne[:, :], tl0, 1.0, None, ALU.min))
            link(dve.tensor_tensor_scan(ordn[:, :], one, ne[:, :], 0.0, ALU.mult, ALU.add))
            total = cum[r0, E - 1:E]
            link(dve.tensor_tensor(alt[:, :], const("io")[r0, 0:E], ordn[:, :], ALU.subtract))
            link(dve.tensor_scalar(alt[:, :], alt[:, :], total, 1.0, ALU.add, ALU.add))
            link(dve.scalar_tensor_tensor(zt[:, 0:E], cum0, -1.0, alt[:, :], ALU.add, ALU.subtract))
            link(dve.tensor_tensor(zt[:, 0:E], zt[:, 0:E], ne[:, :], ALU.mult))
            link(dve.tensor_tensor(zt[:, 0:E], zt[:, 0:E], alt[:, :], ALU.add))
            link(dve.tensor_copy(zt[:, E:E + 1], total))
            link(dve.tensor_scalar(tf[:, TB_ZERO:TB_ZERO + E + 1], zt[:, :], float(P), None, ALU.mult))
            steps_c = const("steps")[r0, :]

            def over(v, n):
                return v[r0, :].unsqueeze(1).to_broadcast([1, n, E])

            def per(c, n):
                return c.unsqueeze(2).to_broadcast([1, n, E])

            ge = big3[r0, 0:S * E].rearrange("o (s e) -> o s e", e=E)
            tmp3 = scratch[r0, 6 * D:6 * D + S * E].rearrange("o (s e) -> o s e", e=E)
            link(dve.tensor_tensor(ge, per(steps_c, S), over(cum, S), ALU.is_ge))
            link(dve.tensor_tensor(tmp3, ge, over(ne, S), ALU.mult))
            link(dve.tensor_reduce(tq[:, 0:S], tmp3, AX.X, ALU.add))
            link(dve.tensor_copy(tq[:, S:S + 1], ordn[:, E - 1:E]))
            link(dve.tensor_scalar(tf[:, TB_NEED:TB_NEED + S], tq[:, 0:S], 2.0, None, ALU.add))
            link(dve.tensor_scalar(tqi[:, :], tq[:, :], 1.0, None, ALU.add))
            link(dve.tensor_scalar(tqi[:, :], tqi[:, :], 1, None, ALU.bitwise_and))
            link(dve.tensor_scalar(tf[:, TB_OFF:TB_OFF + S], tqi[:, 0:S], float(WSZ), None, ALU.mult))
            link(dve.tensor_scalar(tf[:, TB_COFF:TB_COFF + 1], tqi[:, S:S + 1], float(WSZ), None, ALU.mult))
            link(dve.tensor_scalar(tf[:, TB_CNEED:TB_CNEED + 1], ordn[:, E - 1:E], 2.0, None, ALU.add))
            link(dve.tensor_scalar(tf[:, TB_JEND:TB_JEND + 1], ordn[:, E - 1:E], 2.0, None, ALU.add))
            o3 = big3[r0, 0:J * E].rearrange("o (s e) -> o s e", e=E)
            link(dve.tensor_tensor(o3, over(ordn, J), per(const("jseq")[r0, :], J), ALU.is_lt))
            link(dve.tensor_reduce(tf[:, TB_ORDER:TB_ORDER + J], o3, AX.X, ALU.add))
            link(dve.tensor_tensor(o3, over(ordn, J), per(const("jseq0")[r0, :], J), ALU.is_le))
            link(dve.tensor_tensor(o3, o3, over(tl, J), ALU.mult))
            link(dve.tensor_reduce(tf[:, TB_FIN:TB_FIN + J], o3, AX.X, ALU.add))
            ev = big3[r0, 0:S // 2]
            link(dve.tensor_scalar(ev, const("even")[r0, :], total, None, ALU.is_lt))
            link(dve.tensor_reduce(tq[:, 0:1], ev, AX.X, ALU.add))
            link(dve.tensor_scalar(tf[:, TB_ITERS:TB_ITERS + 1], tq[:, 0:1], -2.0, None, ALU.add))
            link(dve.tensor_copy(tf[:, TB_PAR:TB_PAR + J + 2], const("par")[r0, :]))
            dve.tensor_copy(ti[:, :], tf[:, :]).then_inc(s_tab, 1)

            def lows(sec, i, j):
                dve.wait_ge(q[sec, "xhi"], i * 2 + (j + 1))
                dve.tensor_tensor(xtlo[:, j, :], bank[j][:, :], xthi[:, j, :].bitcast(F32),
                                  ALU.subtract).then_inc(q[sec, "xlo"], 1)

            def offsets(sec, i, j, first):
                if not first:
                    dve.wait_ge(s_scat[j] if sec == "A" else s_gath[j], i * 32)
                for k in range(2):
                    dve.tensor_copy(idx[j][k][:, :], pos[:, bass.ds(i * 2 + j, 1), k]).then_inc(q[sec, "idx"], 1)

            def finish(sec, i, j, first):
                dve.wait_ge(q[sec, "dn"], i * 2 + (j + 1))
                xt = x_all[:, bass.ds(i * 2 + j, 1), :].rearrange("p a d -> p (a d)")
                if sec == "A":
                    dve.tensor_tensor(tmpa[:, j, :], bank[5 + j][:, :], mods[:, 5, :],
                                      ALU.mult).then_inc(q["A", "y"], 1)
                    dve.wait_ge(q["A", "y"], i * 2 + (j + 1))
                    dve.tensor_tensor(xt, xt, tmpa[:, j, :], ALU.add).then_inc(q["A", "g8"], 1)
                if sec == "C":
                    y, n = ybuf[:, j, :], i * 2 + (j + 1)
                    dve.wait_ge(s_gath[j], i * 32 + 32)
                    if not first:
                        dve.wait_ge(q["C", "ydma"][j], i * 16)
                    w = [wts[:, bass.ds(i * 2 + j, 1), k] for k in range(2)]
                    dve.scalar_tensor_tensor(y, tbuf[:, j, :], w[0], bank[5 + j][:, :],
                                             ALU.mult, ALU.add).then_inc(q["C", "y"], 1)
                    dve.wait_ge(q["C", "y"], n)
                    dve.scalar_tensor_tensor(y, xtf[:, j, :], w[1], y, ALU.mult, ALU.add).then_inc(s_c2, 1)
                    dve.wait_ge(s_c2, n)
                    dve.tensor_tensor(y, y, mods[:, 5, :], ALU.mult).then_inc(s_c3, 1)
                    dve.wait_ge(s_c3, n)
                    dve.tensor_tensor(y, y, xt, ALU.add).then_inc(s_c4, 1)

            def section(sec):
                def step(i, j, first, last):
                    if sec == "A" and not (isinstance(i, int) and i == NP - 1):
                        offsets("A", i + 1, j, False)
                    if sec == "C" and not first and not last:
                        offsets("C", i + j, 1 - j, False)
                    if not last:
                        if not first:
                            dve.wait_ge(q[sec, "up"], i * 2 + j)
                        lows(sec, i + j, 1 - j)
                    dve.wait_ge(q[sec, "silu"], i * 2 + (j + 1))
                    dve.wait_ge(q[sec, "up"], i * 2 + (j + 1))
                    if not first:
                        dve.wait_ge(q[sec, "gt"], i * 2 + j)
                    dve.tensor_tensor(gbuf[:, 0:F], s1, bank[3][:, 0:F], ALU.mult).then_inc(q[sec, "g"], 1)
                    dve.wait_ge(q[sec, "ghi"], i * 2 + (j + 1))
                    if not first:
                        dve.wait_ge(q[sec, "dn"], i * 2 + j)
                    dve.tensor_tensor(gtl[:, 0:FP], bank[4][:, 0:FP], gth[:, 0:FP].bitcast(F32),
                                      ALU.subtract).then_inc(q[sec, "glo"], 1)
                    if not first and sec != "B":
                        finish(sec, i - 1 + j, 1 - j, isinstance(i, int) and i <= 1 - j)
                return step

            dve.wait_ge(s_at, NP)
            dve.wait_ge(s_stp, NP)
            for j in range(2):
                offsets("A", 0, j, True)
            lows("A", 0, 0)
            steps(dve, NP, section("A"))
            finish("A", NP - 1, 1, False)
            iters = pairs_of_b(dve)
            lows("B", 0, 0)
            steps(dve, iters, section("B"))
            for j in range(2):
                dve.wait_ge(q["B", "ydma"][j], iters * 16)
            for j in range(2):
                offsets("C", 0, j, True)
            lows("C", 0, 0)
            steps(dve, NP, section("C"))
            finish("C", NP - 1, 1, False)


def kernel(L0_attn_x, L0_attn_B, L0_attn_C, L0_attn_D, L0_ffn_gate_w, L0_ffn_router_bias, L0_ffn_W1,
           L0_ffn_W3, L0_ffn_W2, L0_ffn_sw1, L0_ffn_sw3, L0_ffn_sw2, L0_c, L0_wmod):
    import numpy as np
    import concourse.bacc as bacc
    from concourse.bass_utils import run_bass_kernel_spmd

    f = np.float32

    def chunks(a):
        return a.reshape(-1, P, a.shape[1]).transpose(1, 0, 2)

    packed = np.zeros((E + 2, P, WSZ), f)

    def pack(n, w1, w3, w2):
        packed[n, :, :WDN] = np.concatenate([chunks(w1), chunks(w3)], axis=2).reshape(P, WDN)
        w2p = np.zeros((FP, D), f)
        w2p[:F] = w2
        packed[n, :, WDN:] = chunks(w2p).reshape(P, KF * D)

    W1, W3, W2 = (np.asarray(a) for a in (L0_ffn_W1, L0_ffn_W3, L0_ffn_W2))
    s1, s3, s2 = (np.asarray(a) for a in (L0_ffn_sw1, L0_ffn_sw3, L0_ffn_sw2))
    for e in range(E):
        pack(e, W1[e], W3[e], W2[e])
    for n, h in ((SHARED_A, slice(0, F)), (SHARED_B, slice(F, 2 * F))):
        pack(n, s1[h].T, s3[h].T, s2[:, h].T)

    const = np.zeros((P, CW), f)

    def put(name, v):
        const[:, COL[name][0]:COL[name][1]] = v

    put("ident", np.eye(P))
    put("tri", np.triu(np.ones((P, P)), 1))
    put("ones", 1.0)
    put("io", np.tile(np.arange(E), NT))
    put("io8", np.tile(np.arange(E) + E, NT))
    put("steps", np.arange(SMAX))
    put("thr", np.arange(NT) * P)
    put("even", np.arange(SMAX // 2) * 2)
    put("jseq", np.arange(E + 2) + 1)
    put("jseq0", np.arange(E + 2))
    put("par", np.arange(E + 4) % 2 * WSZ)

    arrays = {
        "x": np.asarray(L0_attn_x)[0],
        "ccol": np.asarray(L0_c).reshape(KD, P).T,
        "wmod": np.asarray(L0_wmod),
        "bt": chunks(np.asarray(L0_attn_B).T),
        "ct": chunks(np.asarray(L0_attn_C).T),
        "dvec": np.asarray(L0_attn_D)[None, :],
        "gwt": chunks(np.asarray(L0_ffn_gate_w).T),
        "rb": np.asarray(L0_ffn_router_bias)[None, :],
        "w_all": packed.reshape((E + 2) * P, WSZ),
        "consts": const,
    }
    arrays = {k: np.ascontiguousarray(a) for k, a in arrays.items()}
    nc = bacc.Bacc("TRN2", target_bir_lowering=False, num_devices=1)
    args = [nc.dram_tensor(k, a.shape, mybir.dt.from_np(a.dtype), kind="ExternalInput").ap()
            for k, a in arrays.items()]
    res = nc.dram_tensor("out", (T, D), F32, kind="ExternalOutput").ap()
    build(nc, *args, res)
    r = run_bass_kernel_spmd(nc, [arrays], core_ids=[0])
    return r.results[0]["out"].reshape(1, T, D)
```

```python
from contextlib import ExitStack

import concourse.bass as bass
from concourse import mybir

F32 = mybir.dt.float32
F32R = mybir.dt.float32r
BF16 = mybir.dt.bfloat16
I32 = mybir.dt.int32
U32 = mybir.dt.uint32
ALU = mybir.AluOpType
ACT = mybir.ActivationFunctionType
AX = mybir.AxisListType

P = 128
T, D, N, F, E = 2048, 512, 256, 352, 8
KD, KN = D // P, N // P
NT = T // P
NP = NT // 2
KF = -(-F // P)
FP = KF * P
UP = 2 * F
WSZ = KD * UP + KF * D
WDN = KD * UP
SMAX = 2 * T // P + E
SMIN = 2 * T // P
R = T + P
KR = 20
SHARED_A, SHARED_B = E + 1, E
EPS = 1e-5
BIG = 3.0e38

_sizes = [("ident", P), ("tri", P), ("ones", P), ("io", 2 * E), ("io8", 2 * E), ("eoff", E),
          ("steps", SMAX), ("thr", NT), ("even", SMAX // 2), ("jseq", E + 2), ("jseq0", E + 2),
          ("par", E + 4)]
COL, _at = {}, 0
for _n, _s in _sizes:
    COL[_n] = (_at, _at + _s)
    _at += _s
CW = _at

TB_ROW, TB_OFF, TB_NEED = 0, SMAX, 2 * SMAX
TB_ORDER = 3 * SMAX
TB_FIN = TB_ORDER + E + 2
TB_N = TB_FIN + E + 2
TB_ITERS = TB_N + E
TB_JEND, TB_COFF, TB_CNEED = TB_ITERS + 1, TB_ITERS + 2, TB_ITERS + 3
TB_PAR = TB_ITERS + 4
TBW = TB_PAR + E + 4


def build(nc, x, ccol, wmod, bt, ct, dvec, gwt, rb, w_all, consts, out):
    hs = nc.dram_tensor("hs_rows", (T, D), F32, kind="Internal").ap()
    xs = nc.dram_tensor("xs_rows", (E * R + P, D), F32, kind="Internal").ap()
    ys = nc.dram_tensor("ys_rows", (SMAX * P, D), F32, kind="Internal").ap()

    with ExitStack() as ctx:
        def sb(name, shape, dt=F32):
            return ctx.enter_context(nc.sbuf_tensor(name, shape, dt))

        def sem(name):
            return ctx.enter_context(nc.semaphore(name))

        bank = [ctx.enter_context(nc.psum_tensor(f"bank{i}", [P, 512], F32)) for i in range(8)]

        cst = sb("cst", [P, CW])

        def const(name):
            return cst[:, COL[name][0]:COL[name][1]]

        ident = const("ident")
        tri_b = sb("tri_b", [P, P], BF16)
        ones_b = sb("ones_b", [P, P], BF16)
        x_all = sb("x_all", [P, NT, D])
        whi = sb("whi", [P, 2 * WSZ], F32R)
        wlo = sb("wlo", [P, 2 * WSZ], F32R)
        raw = sb("raw", [P, WSZ])
        mods = sb("mods", [P, 6, D])
        a12 = sb("a12", [P, 2, D])
        bhi = sb("bhi", [P, KD, N], F32R)
        blo = sb("blo", [P, KD, N], F32R)
        chi = sb("chi", [P, KN, D], F32R)
        clo = sb("clo", [P, KN, D], F32R)
        gw = sb("gw", [P, KD, E])
        rbias = sb("rbias", [P, E])
        cols = sb("cols", [P, 2, KD])
        bsa = sb("bsa", [P, KN])
        c_in = sb("c_in", [P, KD])
        sil = sb("sil", [P, KD])
        eps_t = sb("eps_t", [P, 2])
        mhalf = sb("mhalf", [P, 2])
        zrow = sb("zrow", [P, D])
        tbuf = sb("tbuf", [P, 2, D])
        tmpa = sb("tmpa", [P, 2, D])
        h2 = sb("h2", [P, 2, D])
        thi = sb("thi", [P, KD, 2 * P], F32R)
        tlo = sb("tlo", [P, KD, 2 * P], F32R)
        st = sb("st", [P, KN, 2 * P])
        shi = sb("shi", [P, KN, 2 * P], F32R)
        slo = sb("slo", [P, KN, 2 * P], F32R)
        xtf = sb("xtf", [P, 2, D])
        bn1 = sb("bn1", [P, 2, 6])
        bn2 = sb("bn2", [P, 2, 6])
        mv1 = sb("mv1", [P, 2, 2])
        mv2 = sb("mv2", [P, 2, 2])
        ve1 = sb("ve1", [P, 2])
        ve2 = sb("ve2", [P, 2])
        rs1 = sb("rs1", [P, 2])
        rs2 = sb("rs2", [P, 2])
        sc = sb("sc", [P, NT, E])
        oh = [sb("oh1", [P, NT, E]), sb("oh2", [P, NT, E])]
        sel = sb("sel", [P, 2, E])
        ra = sb("ra", [P, 2, E])
        rc = sb("rc", [P, 2, E])
        rm = sb("rm", [P, 2])
        ri = sb("ri", [P, 2])
        mask = sb("mask", [P, 2, E], BF16)
        rbase = sb("rbase", [P, E])
        idx4 = sb("idx4", [P, 4], U32)
        sw = sb("sw", [P, 2, NT])
        den = sb("den", [P, NT])
        wts = sb("wts", [P, NT, 2])
        pos = sb("pos", [P, NT, 2])
        nE = sb("nE", [P, E])
        idx = [[sb(f"idx{j}{k}", [P, 1], U32) for k in range(2)] for j in range(2)]
        tf = sb("tf", [1, TBW])
        ti = sb("ti", [1, TBW], I32)
        tl = sb("tl", [P, E])
        cum = sb("cum", [P, E])
        base = sb("base", [P, E])
        ne = sb("ne", [1, E])
        rmt = sb("rmt", [1, E])
        ordn = sb("ordn", [1, E])
        tq = sb("tq", [1, SMAX + 1])
        tqi = sb("tqi", [1, SMAX + 1], I32)
        xah, xal = sb("xah", [P, 2, D], F32R), sb("xal", [P, 2, D], F32R)
        xbh = thi[:, :, :].rearrange("p a b -> p (a b)").rearrange("p (b d) -> p b d", b=2)
        xbl = tlo[:, :, :].rearrange("p a b -> p (a b)").rearrange("p (b d) -> p b d", b=2)
        s1 = sb("s1", [P, F])
        gbuf = sb("gbuf", [P, FP])
        gth, gtl = sb("gth", [P, FP], F32R), sb("gtl", [P, FP], F32R)
        big3 = sb("big3", [P, SMAX * E + 8])
        xin = h2
        ybuf = tmpa
        hrow = mods[:, 0:2, :]
        fbuf = mods[:, 2, :]
        btr = raw[:, 0:KD * N].rearrange("p (k n) -> p k n", k=KD)
        ctr = raw[:, 1024:1024 + KN * D].rearrange("p (k n) -> p k n", k=KN)
        cga = raw[:, 2048:2048 + KN * D].rearrange("p (k n) -> p k n", k=KN)
        dbc = raw[:, 3072:3072 + D]
        silb = tmpa[:, 0, :].rearrange("p (k m) -> p k m", k=KD)
        ring = x_all[:, NT // 2:, :].rearrange("p (r k) n -> p r k n", r=2)

        l_small = sem("l_small")
        l_attn = sem("l_attn")
        l_x = [sem(f"l_x{g}") for g in range(4)]
        l_wm = [sem(f"l_wm{j}") for j in range(2)]
        s_sil = sem("s_sil")
        s_silb = sem("s_silb")
        s_mod = sem("s_mod")
        s_modc = sem("s_modc")
        s_colT = sem("s_colT")
        s_cols = sem("s_cols")
        s_bsaT = sem("s_bsaT")
        s_fold = sem("s_fold")
        s_rawfree = sem("s_rawfree")
        s_cst = sem("s_cst")
        chain = sem("chain")
        pchain = sem("pchain")
        s_bn1, s_st1, s_rs1, s_ve1 = sem("s_bn1"), sem("s_st1"), sem("s_rs1"), sem("s_ve1")
        s_bn2, s_st2, s_rs2, s_ve2 = sem("s_bn2"), sem("s_st2"), sem("s_rs2"), sem("s_ve2")
        s_t = sem("s_t")
        s_tT = sem("s_tT")
        s_thi = sem("s_thi")
        s_tlo = sem("s_tlo")
        s_stp = sem("s_stp")
        s_tanh = sem("s_tanh")
        s_shi = sem("s_shi")
        s_slo = sem("s_slo")
        s_xa, s_xb, s_xd = sem("s_xa"), sem("s_xb"), sem("s_xd")
        s_at = sem("s_at")
        s_x1 = sem("s_x1")
        s_u = sem("s_u")
        s_h2 = sem("s_h2")
        s_nat = sem("s_nat")
        s_h2T = sem("s_h2T")
        s_xtf = sem("s_xtf")
        s_gate = sem("s_gate")
        s_sc = sem("s_sc")
        s_rt = sem("s_rt")
        s_hrow = sem("s_hrow")
        s_fa = sem("s_fa")
        s_scat = sem("s_scat")
        s_rank = sem("s_rank")
        s_pos = sem("s_pos")
        s_tab = sem("s_tab")
        s_pad = sem("s_pad")
        w_hi, w_raw, w_ready = sem("w_hi"), sem("w_raw"), sem("w_ready")
        q = {}
        for sec in "ABC":
            for n in ("xt", "xhi", "xlo", "up", "silu", "g", "gt", "ghi", "glo", "dn", "y", "idx", "g8"):
                q[sec, n] = sem(f"{n}_{sec}")
            q[sec, "xin"] = [sem(f"xin{j}_{sec}") for j in range(2)]
            q[sec, "ydma"] = [sem(f"ydma{j}_{sec}") for j in range(2)]
        s_gath = [sem(f"s_gath{j}") for j in range(2)]
        s_c2, s_c3, s_c4 = sem("s_c2"), sem("s_c3"), sem("s_c4")

        block = ctx.enter_context(nc.Block())
        WM = [1, 0, 2, 4, 3, 5]

        def iterations(eng, body):
            for it in range(4):
                body(it, it, it)
            with eng.Fori(4, NP) as it:
                body(it, 4, NP - 1)
            for it in range(NP, NP + 4):
                body(it, it, it)

        at = [0]

        def value(eng, v):
            if isinstance(v, int):
                return v
            at[0] += 1
            reg = eng.alloc_register(f"value{at[0]}")
            eng.reg_mov(reg, v)
            return reg

        def pairs_of_b(eng):
            return eng.value_load(ti[0:1, TB_ITERS:TB_ITERS + 1], min_val=NP - 2, max_val=SMAX // 2 - 2) + 2

        def live(lag, lo, hi):
            return lo - lag >= 0 and hi - lag < NP

        def steps(eng, count, step):
            for j in range(2):
                step(0, j, j == 0, False)
            with eng.Fori(1, count - 1) as i:
                for j in range(2):
                    step(i, j, False, False)
            for j in range(2):
                step(count - 1, j, False, j == 1)

        @block.sync
        def _(sp):
            wm_v = wmod.rearrange("(k p) (j n) -> j p k n", p=P, j=6)
            x_v = x.rearrange("(g b p) d -> g p b d", b=4, p=P)

            def piece(i):
                if i >= 2:
                    sp.wait_ge(s_mod, i - 1)
                sp.dma_start(ring[:, i % 2, :, :], wm_v[WM[i]]).then_inc(l_wm[i % 2], 16)

            def tiles(g):
                sp.dma_start(x_all[:, 4 * g:4 * g + 4, :], x_v[g]).then_inc(l_x[g], 16)

            sp.dma_start(c_in[:, :], ccol).then_inc(l_small, 16)
            sp.dma_start(cst[:, :], consts).then_inc(l_small, 16)
            sp.dma_start(gw[:, :, :], gwt).then_inc(l_small, 16)
            sp.dma_start(rbias[:, :], rb.to_broadcast([P, E])).then_inc(l_small, 16)
            piece(0)
            piece(1)
            sp.dma_start(btr, bt).then_inc(l_attn, 16)
            sp.dma_start(dbc, dvec.to_broadcast([P, D])).then_inc(l_attn, 16)
            sp.dma_start(ctr, ct).then_inc(l_attn, 16)
            tiles(0)
            for i in range(2, 6):
                piece(i)
            tiles(1)
            sp.wait_ge(s_mod, 6)
            for g in range(2, 4):
                tiles(g)
            sp.wait_ge(pchain, 3)
            sp.dma_start(ys[SMIN * P:, :].rearrange("(s p) d -> p s d", p=P),
                         zrow[:, :].unsqueeze(1).to_broadcast([P, SMAX - SMIN, D])).then_inc(s_pad, 16)
            sp.dma_start(xs[E * R:, :], zrow[:, :]).then_inc(s_pad, 16)

            def body(it, lo, hi):
                if live(4, lo, hi):
                    p = it - 4
                    left = value(sp, p * 64)
                    sp.wait_ge(s_nat, p * 16 + 16)
                    if lo > 4 or hi > lo:
                        sp.wait_ge(s_scat, left)
                    sp.dma_start(hrow, hs[bass.ds(p * 2 * P, 2 * P), :].rearrange("(b p) d -> p b d", p=P)
                                 ).then_inc(s_hrow, 16)
                if live(2, lo, hi):
                    p = it - 2
                    sp.wait_ge(s_h2, p * 2 + 2)
                    sp.dma_start(hs[bass.ds(p * 2 * P, 2 * P), :].rearrange("(b p) d -> p b d", p=P),
                                 h2[:, :, :]).then_inc(s_nat, 16)

            sp.wait_ge(s_fold, 1)
            iterations(sp, body)

            def load(sec, j, row):
                src = xs if sec == "B" else hs
                sp.dma_start(xin[:, j, :], src[bass.ds(row, P), :]).then_inc(q[sec, "xin"][j], 16)

            sp.wait_ge(s_tab, 1)
            for e in range(E):
                n = sp.value_load(ti[0:1, TB_N + e:TB_N + e + 1], min_val=0, max_val=T)
                sp.dma_start(xs[bass.ds(n + e * R, P), :], zrow[:, :]).then_inc(s_pad, 16)
            sp.wait_ge(s_pad, 16 * (E + 2))
            sp.wait_ge(s_scat, 64 * NP)

            def row_of(n):
                return sp.value_load(ti[0:1, bass.ds(n + TB_ROW, 1)], min_val=0, max_val=E * R)

            iters = pairs_of_b(sp)
            sp.wait_ge(s_h2T, NP)
            for j in range(2):
                load("B", j, row_of(j))

            def stream(sec, count, store):
                def tile_row(n, row):
                    return row_of(n) if sec == "B" else row

                def part(i, j, first):
                    m = 1 - j
                    row = tile_row(i * 2 + (j + 3), i * (2 * P) + (j + 3) * P)
                    sp.wait_ge(q[sec, "xt"], i * 2 + (j + 2))
                    load(sec, m, row)
                    if not first:
                        store(i - 1 + j, m)

                sp.wait_ge(q[sec, "xt"], 1)
                load(sec, 0, tile_row(2, 2 * P))
                part(0, 0, True)
                part(0, 1, False)
                with sp.Fori(1, count - 2) as i:
                    for j in range(2):
                        part(i, j, False)
                part(count - 2, 0, False)
                store(count - 2, 0)
                store(count - 2, 1)
                for j in range(2):
                    store(count - 1, j)

            def store_y(i, j):
                sp.wait_ge(q["B", "y"], i * 2 + (j + 1))
                sp.dma_start(ys[bass.ds(i * (2 * P) + j * P, P), :], ybuf[:, j, :]).then_inc(q["B", "ydma"][j], 16)

            stream("B", iters, store_y)

            sp.wait_ge(q["B", "xt"], iters * 2)
            for j in range(2):
                load("C", j, j * P)

            def store_out(i, j):
                sp.wait_ge(s_c4, i * 2 + (j + 1))
                sp.dma_start(out[bass.ds(i * (2 * P) + j * P, P), :], ybuf[:, j, :]).then_inc(q["C", "ydma"][j], 16)

            stream("C", NP, store_out)
            for j in range(2):
                sp.wait_ge(q["C", "ydma"][j], 16 * NP)

        @block.gpsimd
        def _(pool):
            pool.memset(eps_t[:, :], EPS).then_inc(pchain, 1)
            pool.memset(mhalf[:, :], -0.5).then_inc(pchain, 1)
            pool.memset(zrow[:, :], 0.0).then_inc(pchain, 1)
            pool.wait_ge(pchain, 3)

            def fetch(row, off, slot_free):
                pool.dma_start(raw[:, :], w_all[bass.ds(row * P, P), :]).then_inc(w_raw, 16)
                slot_free()
                pool.dma_start(whi[:, bass.ds(off, WSZ)], w_all[bass.ds(row * P, P), :],
                               max_dma_last_dim=8192).then_inc(w_hi, 16)

            def low_part(n, off, part):
                if part == 0:
                    pool.wait_ge(w_raw, n * 16 + 16)
                    pool.wait_ge(w_hi, n * 16 + 16)
                a, w = part * (WSZ // 4), WSZ // 4
                ins = pool.tensor_tensor(wlo[:, off + a:off + a + w], raw[:, a:a + w],
                                         whi[:, off + a:off + a + w].bitcast(F32), ALU.subtract)
                if part == 3:
                    ins.then_inc(w_ready, 1)

            def low(n, off):
                pool.wait_ge(w_raw, n * 16 + 16)
                pool.wait_ge(w_hi, n * 16 + 16)
                pool.tensor_tensor(wlo[:, bass.ds(off, WSZ)], raw[:, :],
                                   whi[:, bass.ds(off, WSZ)].bitcast(F32), ALU.subtract).then_inc(w_ready, 1)

            def body(it, lo, hi):
                if live(1, lo, hi):
                    p = it - 1
                    pool.wait_ge(s_t, p * 2 + 2)
                    for j in range(2):
                        pool.tensor_tensor(tmpa[:, j, :], tbuf[:, j, :], a12[:, 0, :], ALU.mult).then_inc(s_xa, 1)
                    pool.wait_ge(s_xa, p * 2 + 2)
                    for j in range(2):
                        pool.tensor_tensor(tmpa[:, j, :], tmpa[:, j, :], a12[:, 1, :], ALU.add).then_inc(s_xb, 1)
                    pool.wait_ge(s_xb, p * 2 + 2)
                    xp = x_all[:, bass.ds(p * 2, 2), :]
                    pool.tensor_tensor(xp, xp, tmpa[:, :, :], ALU.add).then_inc(s_xd, 1)
                if live(2, lo, hi):
                    p = it - 2
                    pool.wait_ge(s_st2, p * 2 + 2)
                    pool.tensor_tensor(ve2[:, :], mv2[:, :, 1], eps_t[:, :], ALU.add).then_inc(s_ve2, 1)
                    pool.wait_ge(s_ve2, p + 1)
                    if lo > 2:
                        pool.wait_ge(s_h2, p * 2)
                    pool.tensor_tensor(rs2[:, :], ve2[:, :], mhalf[:, :], ALU.pow).then_inc(s_rs2, 1)
                if live(0, lo, hi):
                    pool.wait_ge(s_st1, it * 2 + 2)
                    pool.tensor_tensor(ve1[:, :], mv1[:, :, 1], eps_t[:, :], ALU.add).then_inc(s_ve1, 1)
                    pool.wait_ge(s_ve1, it + 1)
                    if lo > 0:
                        pool.wait_ge(s_t, it * 2)
                    pool.tensor_tensor(rs1[:, :], ve1[:, :], mhalf[:, :], ALU.pow).then_inc(s_rs1, 1)
                for stage, j in ((4, 1), (3, 0)):
                    if live(stage, lo, hi):
                        p = it - stage
                        pool.wait_ge(q["A", "y"], p * 2 + (j + 1))
                        xt = x_all[:, bass.ds(p * 2 + j, 1), :].rearrange("p a d -> p (a d)")
                        pool.tensor_tensor(xt, xt, fbuf, ALU.add).then_inc(s_fa, 1)
                if live(4, lo, hi):
                    p = it - 4
                    landed, known = value(pool, p * 16 + 16), value(pool, p * KR + KR)
                    pool.wait_ge(s_fold, 1)
                    pool.wait_ge(s_hrow, landed)
                    pool.wait_ge(s_rt, known)
                    for j in range(2):
                        for k in range(2):
                            pool.indirect_dma_start(
                                xs[:, :], bass.IndirectOffsetOnAxis(ap=idx4[:, 2 * j + k:2 * j + k + 1], axis=0),
                                hrow[:, j, :], None).then_inc(s_scat, 16)
                if lo in (1, 2):
                    low_part(0, 0, 2 * lo - 2)
                    low_part(0, 0, 2 * lo - 1)
                if lo == hi == 3:
                    pool.wait_ge(w_ready, 1)
                    fetch(0, WSZ, lambda: None)
                if lo >= NP:
                    low_part(1, WSZ, lo - NP)

            pool.wait_ge(s_fold, 1)
            pool.wait_ge(s_mod, 6)
            fetch(SHARED_A, 0, lambda: None)
            iterations(pool, body)

            def table(at, low_, high_):
                return pool.value_load(ti[0:1, bass.ds(at, 1)], min_val=low_, max_val=high_)

            pool.wait_ge(s_tab, 1)
            jend = table(TB_JEND, 3, E + 2)
            with pool.Fori(2, jend) as n:
                row = table(n + (TB_ORDER - 1), 0, E)
                fin = table(n + (TB_FIN - 2), 0, SMAX)
                off = table(n + (TB_PAR), 0, WSZ)
                pool.wait_ge(w_ready, n)
                fetch(row, off, lambda: (pool.wait_ge(q["A", "dn"], NT), pool.wait_ge(q["B", "dn"], fin)))
                low(n, off)
            iters = pairs_of_b(pool)
            stored = value(pool, iters * 16)
            pool.wait_ge(s_tab, 1)
            for j in range(2):
                pool.wait_ge(q["B", "ydma"][j], stored)

            def gather(i, j, first):
                known, used = value(pool, i * 4 + (2 * j + 2)), None if first else value(pool, i * 2 + (j - 1))
                pool.wait_ge(s_tab, 1)
                pool.wait_ge(q["C", "idx"], known)
                if not first:
                    pool.wait_ge(s_c2, used)
                for k, dst in ((0, tbuf), (1, xtf)):
                    pool.indirect_dma_start(dst[:, j, :], None, ys[:, :],
                                            bass.IndirectOffsetOnAxis(ap=idx[j][k][:, :], axis=0)
                                            ).then_inc(s_gath[j], 16)

            for j in range(2):
                gather(0, j, True)
            with pool.Fori(1, NP) as i:
                for j in range(2):
                    gather(i, j, False)

        @block.scalar
        def _(act):
            def hidden(p, j, lo):
                n = p * 2 + (j + 1)
                act.wait_ge(q["A", "up"], n)
                if lo > 3 or j:
                    act.wait_ge(q["A", "g"], p * 2 + j)
                act.activation(s1[:, :], bank[2][:, 0:F], ACT.Silu).then_inc(q["A", "silu"], 1)
                act.wait_ge(q["A", "gt"], n)
                if lo > 3 or j:
                    act.wait_ge(q["A", "dn"], p * 2 + j)
                act.activation(gth[:, :], bank[4 + j][:, 0:FP], ACT.Copy).then_inc(q["A", "ghi"], 1)

            def body(it, lo, hi):
                if live(1, lo, hi):
                    p = it - 1
                    act.wait_ge(s_tT, p + 1)
                    if lo > 1:
                        act.wait_ge(s_stp, p)
                    for j in range(2):
                        act.activation(thi[:, :, j * P:j * P + P],
                                       bank[2 + j][:, :].rearrange("p (k m) -> p k m", k=KD),
                                       ACT.Copy).then_inc(s_thi, 1)
                if live(3, lo, hi):
                    p = it - 3
                    act.wait_ge(s_h2T, p + 1)
                    if lo > 3:
                        act.wait_ge(q["A", "up"], p * 2)
                        act.wait_ge(s_gate, p)
                    for j in range(2):
                        act.activation(xah[:, j, :], bank[4 + j][:, :], ACT.Copy).then_inc(q["A", "xhi"], 1)
                        act.activation(xtf[:, j, :], bank[4 + j][:, :], ACT.Copy).then_inc(s_xtf, 1)
                    hidden(p, 0, lo)
                if live(1, lo, hi):
                    p = it - 1
                    act.wait_ge(s_stp, p + 1)
                    if lo > 1:
                        act.wait_ge(s_slo, p)
                    for n in range(KN):
                        act.activation(st[:, n, :], bank[6][:, n * 2 * P:(n + 1) * 2 * P], ACT.Tanh,
                                       bias=bsa[:, n:n + 1]).then_inc(s_tanh, 1)
                    act.wait_ge(s_tanh, p * 2 + 2)
                    if lo > 1:
                        act.wait_ge(s_at, p)
                    act.activation(shi[:, :, :], st[:, :, :], ACT.Copy).then_inc(s_shi, 1)
                if live(3, lo, hi):
                    p = it - 3
                    hidden(p, 1, lo)
                    act.wait_ge(s_gate, p + 1)
                    act.activation(sc[:, bass.ds(p * 2, 2), :],
                                   bank[7][:, 0:2 * E].rearrange("p (b e) -> p b e", b=2),
                                   ACT.Sigmoid).then_inc(s_sc, 1)

            act.wait_ge(l_small, 64)
            act.activation(sil[:, :], c_in[:, :], ACT.Silu).then_inc(s_sil, 1)
            act.wait_ge(s_fold, 1)
            iterations(act, body)

            def high(sec, i, j):
                act.wait_ge(q[sec, "xt"], i * 2 + (j + 1))
                act.activation(xbh[:, j, :], bank[j][:, :], ACT.Copy).then_inc(q[sec, "xhi"], 1)

            def result(i, j, first):
                act.wait_ge(q["B", "dn"], i * 2 + (j + 1))
                if not first:
                    act.wait_ge(q["B", "ydma"][j], i * 16)
                act.activation(ybuf[:, j, :], bank[5 + j][:, :], ACT.Copy).then_inc(q["B", "y"], 1)

            def section(sec):
                def step(i, j, first, last):
                    if not last:
                        if not first:
                            act.wait_ge(q[sec, "up"], i * 2 + j)
                        high(sec, i + j, 1 - j)
                    act.wait_ge(q[sec, "up"], i * 2 + (j + 1))
                    if not first:
                        act.wait_ge(q[sec, "g"], i * 2 + j)
                    act.activation(s1[:, :], bank[2][:, 0:F], ACT.Silu).then_inc(q[sec, "silu"], 1)
                    act.wait_ge(q[sec, "gt"], i * 2 + (j + 1))
                    if not first:
                        act.wait_ge(q[sec, "dn"], i * 2 + j)
                    act.activation(gth[:, :], bank[4][:, 0:FP], ACT.Copy).then_inc(q[sec, "ghi"], 1)
                    if sec == "B" and not first:
                        result(i - 1 + j, 1 - j, isinstance(i, int) and i <= 1 - j)
                return step

            act.wait_ge(s_stp, NP)
            act.wait_ge(s_tab, 1)
            iters = pairs_of_b(act)
            high("B", 0, 0)
            steps(act, iters, section("B"))
            result(iters - 1, 1, False)
            act.wait_ge(q["B", "g"], iters * 2)
            high("C", 0, 0)
            steps(act, NP, section("C"))

        @block.tensor
        def _(pe):
            def product(dst, pairs):
                n = len(pairs)
                for m, (ah, al, bh, bl) in enumerate(pairs):
                    pe.matmul(dst, ah, bh, start=(m == 0), stop=False)
                    pe.matmul(dst, ah, bl, start=False, stop=False)
                    mm = pe.matmul(dst, al, bh, start=False, stop=(m == n - 1))
                return mm

            pe.wait_ge(s_silb, KD)
            for i in range(6):
                pe.wait_ge(l_wm[i % 2], 16 * (i // 2 + 1))
                if i >= 2:
                    pe.wait_ge(s_modc, i - 1)
                for k in range(KD):
                    mm = pe.matmul(bank[i % 2][:, :], silb[:, k, :], ring[:, i % 2, k, :],
                                   start=(k == 0), stop=(k == KD - 1))
                mm.then_inc(s_mod, 1)
                if i == 2:
                    pe.wait_ge(s_modc, 2)
                    for j in range(2):
                        for k in range(KD):
                            mm = pe.transpose(bank[4 + j][:, k * P:(k + 1) * P],
                                              mods[:, j, k * P:(k + 1) * P], ident)
                    mm.then_inc(s_colT, 1)
                    pe.wait_ge(s_cols, 1)
                    pe.wait_ge(l_attn, 48)
                    for n in range(KN):
                        for k in range(KD):
                            mm = pe.matmul(bank[6][:, n:n + 1], btr[:, k, n * P:(n + 1) * P],
                                           cols[:, 0, k:k + 1], start=(k == 0), stop=(k == KD - 1))
                    mm.then_inc(s_bsaT, 1)

            def transposes(dst, src):
                for k in range(KD):
                    mm = pe.transpose(dst[:, k * P:(k + 1) * P], src[:, k * P:(k + 1) * P], ident)
                return mm

            def up(sec, i, j, off):
                xh, xl = (xah, xal) if sec == "A" else (xbh, xbl)
                pe.wait_ge(q[sec, "xlo"], i * 2 + (j + 1))
                for m in range(KD):
                    a = slice(m * P, (m + 1) * P)
                    for h in range(2):
                        w = off + (m * UP + h * F)
                        wh, wl = whi[:, bass.ds(w, F)], wlo[:, bass.ds(w, F)]
                        dst = bank[2 + h][:, 0:F]
                        pe.matmul(dst, xh[:, j, a], wh, start=(m == 0), stop=False)
                        pe.matmul(dst, xh[:, j, a], wl, start=False, stop=False)
                        mm = pe.matmul(dst, xl[:, j, a], wh, start=False, stop=(m == KD - 1))
                mm.then_inc(q[sec, "up"], 1)

            def down(sec, i, j, off, bank_used, to):
                pe.wait_ge(q[sec, "glo"], i * 2 + (j + 1))
                if bank_used:
                    pe.wait_ge(q[sec, "y"], i * 2 + (j - 1))
                for m in range(KF):
                    a = slice(m * P, (m + 1) * P)
                    w = off + (WDN + m * D)
                    wh, wl = whi[:, bass.ds(w, D)], wlo[:, bass.ds(w, D)]
                    dst = bank[to + j][:, :]
                    pe.matmul(dst, gth[:, a], wh, start=(m == 0), stop=False)
                    pe.matmul(dst, gth[:, a], wl, start=False, stop=False)
                    mm = pe.matmul(dst, gtl[:, a], wh, start=False, stop=(m == KF - 1))
                mm.then_inc(q[sec, "dn"], 1)

            def turn_g(dst):
                for m in range(KF):
                    mm = pe.transpose(dst[:, m * P:(m + 1) * P], gbuf[:, m * P:(m + 1) * P], ident)
                return mm

            def body(it, lo, hi):
                if live(1, lo, hi):
                    p = it - 1
                    pe.wait_ge(s_t, p * 2 + 2)
                    if lo > 1:
                        pe.wait_ge(s_tlo, p * 2)
                    if lo > 3:
                        pe.wait_ge(q["A", "g"], (it - 4) * 2 + 2)
                    for j in range(2):
                        mm = transposes(bank[2 + j], tbuf[:, j, :])
                    mm.then_inc(s_tT, 1)
                if live(3, lo, hi):
                    p = it - 3
                    pe.wait_ge(s_h2, p * 2 + 2)
                    if lo > 3:
                        pe.wait_ge(q["A", "glo"], p * 2)
                    for j in range(2):
                        mm = transposes(bank[4 + j], h2[:, j, :])
                    mm.then_inc(s_h2T, 1)
                if live(2, lo, hi):
                    p = it - 2
                    pe.wait_ge(s_slo, p + 1)
                    if lo > 2:
                        pe.wait_ge(s_x1, p * 2)
                    if lo > 3:
                        pe.wait_ge(q["A", "y"], (it - 4) * 2 + 1)
                    for j in range(2):
                        t = slice(j * P, (j + 1) * P)
                        mm = product(bank[j][:, :], [(shi[:, n, t], slo[:, n, t], chi[:, n, :], clo[:, n, :])
                                                     for n in range(KN)])
                    mm.then_inc(s_at, 1)
                if live(3, lo, hi):
                    if live(1, lo, hi):
                        pe.wait_ge(s_tlo, (it - 1) * 2 + 2)
                    if lo > 3:
                        pe.wait_ge(q["A", "g"], (it - 3) * 2)
                    up("A", it - 3, 0, 0)
                if live(2, lo, hi):
                    pe.wait_ge(s_x1, (it - 2) * 2 + 2)
                if live(4, lo, hi):
                    if lo > 4 or hi > lo:
                        pe.wait_ge(q["A", "y"], (it - 4) * 2)
                    down("A", it - 4, 1, 0, False, 0)
                if live(3, lo, hi):
                    pe.wait_ge(s_xtf, (it - 3) * 2 + 2)
                    pe.wait_ge(q["A", "g"], (it - 3) * 2 + 1)
                    turn_g(bank[4]).then_inc(q["A", "gt"], 1)
                if live(1, lo, hi):
                    p = it - 1
                    pe.wait_ge(s_thi, p * 2 + 2)
                    pe.wait_ge(s_tlo, p * 2 + 2)
                    if lo > 1:
                        pe.wait_ge(s_tanh, p * 2)
                    for n in range(KN):
                        t = slice(n * P, (n + 1) * P)
                        mm = product(bank[6][:, n * 2 * P:(n + 1) * 2 * P],
                                     [(bhi[:, k, t], blo[:, k, t], thi[:, k, :], tlo[:, k, :]) for k in range(KD)])
                    mm.then_inc(s_stp, 1)
                if live(3, lo, hi):
                    up("A", it - 3, 1, 0)
                if live(4, lo, hi):
                    pe.wait_ge(s_rt, (it - 4) * KR + 13)
                    at_, all_ = 2 * E, 4 * E
                    pe.matmul(bank[7][:, at_:at_ + 2 * E], tri_b[:, :], mask[:, :, :], start=True, stop=False)
                    pe.matmul(bank[7][:, at_ + E:at_ + 2 * E], ones_b[:, :], mask[:, 0, :], start=False, stop=True)
                    pe.matmul(bank[7][:, all_:all_ + E], ones_b[:, :], mask[:, 0, :], start=True, stop=False)
                    pe.matmul(bank[7][:, all_:all_ + E], ones_b[:, :], mask[:, 1, :],
                              start=False, stop=True).then_inc(s_rank, 1)
                if live(3, lo, hi):
                    p = it - 3
                    if lo > 3:
                        pe.wait_ge(q["A", "y"], (it - 4) * 2 + 1)
                    down("A", p, 0, 0, False, 0)
                    pe.wait_ge(q["A", "g"], p * 2 + 2)
                    turn_g(bank[5]).then_inc(q["A", "gt"], 1)
                    if lo > 3:
                        pe.wait_ge(s_sc, p)
                        pe.wait_ge(s_rt, (it - 4) * KR + 15)
                    for j in range(2):
                        for k in range(KD):
                            mm = pe.matmul(bank[7][:, j * E:(j + 1) * E], xtf[:, j, k * P:(k + 1) * P],
                                           gw[:, k, :], start=(k == 0), stop=(k == KD - 1))
                    mm.then_inc(s_gate, 1)
                if lo == hi == 2:
                    pe.wait_ge(w_ready, 1)

            pe.wait_ge(s_modc, 6)
            pe.wait_ge(s_fold, 1)
            iterations(pe, body)

            def turn(sec, i, j):
                pe.wait_ge(q[sec, "xin"][j], i * 16 + 16)
                transposes(bank[j], xin[:, j, :]).then_inc(q[sec, "xt"], 1)

            def section(sec, off_of, look_up=None):
                def step(i, j, first, last):
                    off = off_of(j)
                    if not last:
                        if not first:
                            pe.wait_ge(q[sec, "xlo"], i * 2 + j)
                        turn(sec, i + j, 1 - j)
                    if not first:
                        pe.wait_ge(q[sec, "g"], i * 2 + j)
                    if look_up:
                        pe.wait_ge(w_ready, need)
                    up(sec, i, j, off)
                    if not first:
                        down(sec, i - 1 + j, 1 - j, off_of(1 - j), not (isinstance(i, int) and i <= 1), 5)
                    if look_up and not last:
                        look_up(i * 2 + (j + 1), 1 - j)
                    pe.wait_ge(q[sec, "g"], i * 2 + (j + 1))
                    turn_g(bank[4]).then_inc(q[sec, "gt"], 1)
                return step

            off_b = [pe.alloc_register(f"off_b{j}") for j in range(2)]
            need = pe.alloc_register("need")

            def look_up(n, j):
                pe.reg_mov(off_b[j], pe.value_load(ti[0:1, bass.ds(n + TB_OFF, 1)], min_val=0, max_val=WSZ))
                pe.reg_mov(need, pe.value_load(ti[0:1, bass.ds(n + TB_NEED, 1)], min_val=2, max_val=E + 2))

            pe.wait_ge(s_tab, 1)
            iters = pairs_of_b(pe)
            pe.wait_ge(q["A", "y"], NT)
            pe.wait_ge(q["A", "glo"], NT)
            pe.wait_ge(s_tlo, NT)
            pe.wait_ge(s_tanh, NT)
            turn("B", 0, 0)
            look_up(0, 0)
            def looked_up(j):
                return pe.snap(off_b[j], min_val=0, max_val=WSZ)

            steps(pe, iters, section("B", looked_up, look_up))
            down("B", iters - 1, 1, looked_up(1), True, 5)

            off_c = pe.value_load(ti[0:1, TB_COFF:TB_COFF + 1], min_val=0, max_val=WSZ)
            need_c = pe.value_load(ti[0:1, TB_CNEED:TB_CNEED + 1], min_val=2, max_val=E + 2)
            pe.wait_ge(w_ready, need_c)
            pe.wait_ge(q["B", "y"], iters * 2)
            turn("C", 0, 0)
            steps(pe, NP, section("C", lambda j: off_c))
            down("C", NP - 1, 1, off_c, True, 5)

        @block.vector
        def _(dve):
            count = [0]

            def link(ins):
                count[0] += 1
                ins.then_inc(chain, 1)
                dve.wait_ge(chain, count[0])

            dve.wait_ge(l_small, 64)
            link(dve.tensor_copy(tri_b[:, :], const("tri")))
            link(dve.tensor_copy(ones_b[:, :], const("ones")))
            dve.wait_ge(s_sil, 1)
            for k in range(KD):
                dve.tensor_scalar(silb[:, k, :], const("ones"), sil[:, k:k + 1], None, ALU.mult).then_inc(s_silb, 1)

            t1, t2 = h2[:, 0, :], h2[:, 1, :]
            for i, m in enumerate(WM):
                dve.wait_ge(s_mod, i + 1)
                src, dst = bank[i % 2][:, :], mods[:, m, :]
                if m in (1, 4):
                    dve.tensor_scalar(dst, src, 1.0, None, ALU.add).then_inc(s_modc, 1)
                else:
                    dve.tensor_copy(dst, src).then_inc(s_modc, 1)
                if m in (2, 5):
                    dve.wait_ge(s_modc, i + 1)
                    link(dve.tensor_scalar(t1, dst, 0.0, 2.0, ALU.is_ge, ALU.mult))
                    link(dve.scalar_tensor_tensor(t2, dst, -1.0, dst, ALU.mult, ALU.max))
                    link(dve.tensor_scalar(t2, t2, 0.25, None, ALU.max))
                    link(dve.scalar_tensor_tensor(dst, t1, -1.0, t2, ALU.add, ALU.mult))
                if i == 2:
                    dve.wait_ge(s_modc, 3)
                    dve.wait_ge(s_colT, 1)
                    for j in range(2):
                        cv = bank[4 + j][:, :].rearrange("p (k m) -> p k m", k=KD)[:, :, 0]
                        link(dve.tensor_copy(cols[:, j, :], cv))
                    dve.tensor_copy(t2[:, 0:KD], cols[:, 0, :]).then_inc(s_cols, 1)
                    dve.wait_ge(l_attn, 48)
                    for k in range(KD):
                        link(dve.tensor_scalar(bhi[:, k, :], btr[:, k, :], cols[:, 1, k:k + 1], None, ALU.mult))
                        link(dve.scalar_tensor_tensor(blo[:, k, :], btr[:, k, :], cols[:, 1, k:k + 1],
                                                      bhi[:, k, :].bitcast(F32), ALU.mult, ALU.subtract))
                    for n in range(KN):
                        link(dve.tensor_tensor(cga[:, n, :], ctr[:, n, :], mods[:, 2, :], ALU.mult))
                    link(dve.tensor_copy(chi[:, :, :], cga))
                    link(dve.tensor_tensor(clo[:, :, :], cga, chi[:, :, :].bitcast(F32), ALU.subtract))
                    link(dve.tensor_tensor(a12[:, 0, :], dbc, mods[:, 2, :], ALU.mult))
                    link(dve.tensor_tensor(a12[:, 1, :], a12[:, 0, :], mods[:, 0, :], ALU.mult))
                    link(dve.tensor_tensor(a12[:, 0, :], a12[:, 0, :], mods[:, 1, :], ALU.mult))
                    dve.wait_ge(s_bsaT, 1)
                    dve.tensor_copy(bsa[:, :], bank[6][:, 0:KN]).then_inc(s_fold, 1)
            link(dve.memset(gbuf[:, F:FP], 0.0))
            link(dve.tensor_copy(rbase[:, :], const("eoff")))
            io, io8 = (const(n).rearrange("p (t e) -> p t e", e=E) for n in ("io", "io8"))

            def product_a(p, j, lo):
                n = p * 2 + (j + 1)
                dve.wait_ge(q["A", "silu"], n)
                if lo > 3 or j:
                    dve.wait_ge(q["A", "gt"], p * 2 + j)
                dve.tensor_tensor(gbuf[:, 0:F], s1[:, :], bank[3][:, 0:F], ALU.mult).then_inc(q["A", "g"], 1)

            def low_a(p, j, lo):
                dve.wait_ge(q["A", "ghi"], p * 2 + (j + 1))
                dve.tensor_tensor(gtl[:, :], bank[4 + j][:, 0:FP], gth[:, :].bitcast(F32), ALU.subtract).then_inc(q["A", "glo"], 1)

            def finish_a(p, j, lo):
                dve.wait_ge(q["A", "dn"], p * 2 + (j + 1))
                if lo > 3 or j:
                    dve.wait_ge(s_fa, p * 2 + j)
                dve.tensor_tensor(fbuf, bank[j][:, :], mods[:, 5, :], ALU.mult).then_inc(q["A", "y"], 1)

            def route(it, lo, hi, *which):
                if not live(4, lo, hi):
                    return
                p = it - 4
                pair = bass.ds(p * 2, 2)

                def of_both(t):
                    return t[:, :].unsqueeze(2).to_broadcast([P, 2, E])

                for n in which:
                    if n == 0:
                        dve.wait_ge(s_sc, p + 1)
                        ins = dve.tensor_tensor(sel[:, :, :], sc[:, pair, :],
                                                rbias[:, :].unsqueeze(1).to_broadcast([P, 2, E]), ALU.add)
                    else:
                        dve.wait_ge(s_rt, p * KR + n)
                    k = n // 6
                    if n in (1, 7):
                        ins = dve.tensor_reduce(rm[:, :], sel[:, :, :], AX.X, ALU.max)
                    if n in (2, 8):
                        ins = dve.tensor_tensor(ra[:, :, :], sel[:, :, :], of_both(rm), ALU.is_equal)
                    if n in (3, 9):
                        ins = dve.scalar_tensor_tensor(rc[:, :, :], ra[:, :, :], -float(E), io8, ALU.mult, ALU.add)
                    if n in (4, 10):
                        ins = dve.tensor_reduce(ri[:, :], rc[:, :, :], AX.X, ALU.min)
                    if n in (5, 11):
                        ins = dve.tensor_tensor(oh[k if n == 11 else 0][:, pair, :], io, of_both(ri), ALU.is_equal)
                    if n == 6:
                        ins = dve.scalar_tensor_tensor(sel[:, :, :], oh[0][:, pair, :], -BIG, sel[:, :, :],
                                                       ALU.mult, ALU.add)
                    if n == 12:
                        ins = dve.tensor_tensor(mask[:, :, :], oh[0][:, pair, :], oh[1][:, pair, :], ALU.add)
                    if n == 13:
                        dve.wait_ge(s_rank, p + 1)
                        ins = dve.tensor_tensor(rc[:, :, :], bank[7][:, 2 * E:4 * E].rearrange("p (t e) -> p t e", e=E),
                                                rbase[:, :].unsqueeze(1).to_broadcast([P, 2, E]), ALU.add)
                    if n == 14:
                        ins = dve.tensor_tensor(rbase[:, :], bank[7][:, 4 * E:5 * E], rbase[:, :], ALU.add)
                    if n in (15, 17):
                        ins = dve.tensor_tensor(ra[:, :, :], rc[:, :, :], oh[(n - 15) // 2][:, pair, :], ALU.mult)
                    if n in (16, 18):
                        ins = dve.tensor_reduce(pos[:, pair, (n - 16) // 2], ra[:, :, :], AX.X, ALU.add)
                    if n == 19:
                        if lo > 4 or hi > lo:
                            dve.wait_ge(s_scat, p * 64)
                        ins = dve.tensor_scalar(idx4[:, :].rearrange("p (t k) -> p t k", k=2), pos[:, pair, :],
                                                0.0, None, ALU.add)
                    ins.then_inc(s_rt, 1)

            def body(it, lo, hi):
                if live(1, lo, hi):
                    p = it - 1
                    dve.wait_ge(s_thi, p * 2 + 2)
                    if lo > 1:
                        dve.wait_ge(s_stp, p)
                    for j in range(2):
                        t = slice(j * P, (j + 1) * P)
                        dve.tensor_tensor(tlo[:, :, t], bank[2 + j][:, :].rearrange("p (k m) -> p k m", k=KD),
                                          thi[:, :, t].bitcast(F32), ALU.subtract).then_inc(s_tlo, 1)
                if live(3, lo, hi):
                    p = it - 3
                    for j in range(2):
                        dve.wait_ge(s_xtf, p * 2 + (j + 1))
                        dve.tensor_tensor(xal[:, j, :], bank[4 + j][:, :], xah[:, j, :].bitcast(F32),
                                          ALU.subtract).then_inc(q["A", "xlo"], 1)
                route(it, lo, hi, 0)
                if live(2, lo, hi):
                    p = it - 2
                    dve.wait_ge(s_at, p + 1)
                    dve.wait_ge(s_xd, p + 1)
                    for j in range(2):
                        xt = x_all[:, bass.ds(p * 2 + j, 1), :].rearrange("p a d -> p (a d)")
                        dve.tensor_tensor(xt, bank[j][:, :], xt, ALU.add).then_inc(s_x1, 1)
                route(it, lo, hi, 1)
                if live(0, lo, hi):
                    if lo < 4:
                        dve.wait_ge(l_x[lo // 2], 16)
                    for j in range(2):
                        xt = x_all[:, bass.ds(it * 2 + j, 1), :].rearrange("p a d -> p (a d)")
                        dve.bn_stats(bn1[:, j, :], xt).then_inc(s_bn1, 1)
                route(it, lo, hi, 2)
                if live(2, lo, hi):
                    p = it - 2
                    done = value(dve, p * 2 + 2)
                    dve.wait_ge(s_fold, 1)
                    dve.wait_ge(s_x1, done)
                    for j in range(2):
                        xt = x_all[:, bass.ds(p * 2 + j, 1), :].rearrange("p a d -> p (a d)")
                        dve.bn_stats(bn2[:, j, :], xt).then_inc(s_bn2, 1)
                route(it, lo, hi, 3)
                if live(0, lo, hi):
                    done = value(dve, it * 2 + 2)
                    dve.wait_ge(s_fold, 1)
                    dve.wait_ge(s_bn1, done)
                    for j in range(2):
                        dve.bn_aggr(mv1[:, j, :], bn1[:, j, :]).then_inc(s_st1, 1)
                route(it, lo, hi, 4)
                if live(2, lo, hi):
                    done = value(dve, (it - 2) * 2 + 2)
                    dve.wait_ge(s_fold, 1)
                    dve.wait_ge(s_bn2, done)
                    for j in range(2):
                        dve.bn_aggr(mv2[:, j, :], bn2[:, j, :]).then_inc(s_st2, 1)
                route(it, lo, hi, 5)
                if live(3, lo, hi):
                    product_a(it - 3, 0, lo)
                route(it, lo, hi, 6)
                if live(2, lo, hi):
                    p = it - 2
                    dve.wait_ge(s_st2, p * 2 + 2)
                    if lo > 2:
                        dve.wait_ge(s_h2T, p)
                        dve.wait_ge(s_nat, p * 16)
                    for j in range(2):
                        xt = x_all[:, bass.ds(p * 2 + j, 1), :].rearrange("p a d -> p (a d)")
                        dve.scalar_tensor_tensor(h2[:, j, :], xt, mv2[:, j, 0:1], mods[:, 4, :],
                                                 ALU.subtract, ALU.mult).then_inc(s_u, 1)
                        route(it, lo, hi, 7 + j)
                if live(4, lo, hi):
                    if not live(2, lo, hi):
                        route(it, lo, hi, 7, 8)
                    finish_a(it - 4, 1, lo)
                route(it, lo, hi, 9)
                if live(2, lo, hi):
                    p = it - 2
                    dve.wait_ge(s_rs2, p + 1)
                    dve.wait_ge(s_u, p * 2 + 2)
                    for j in range(2):
                        dve.scalar_tensor_tensor(h2[:, j, :], h2[:, j, :], rs2[:, j:j + 1], mods[:, 3, :],
                                                 ALU.mult, ALU.add).then_inc(s_h2, 1)
                        route(it, lo, hi, 10 + j)
                elif live(4, lo, hi):
                    route(it, lo, hi, 10, 11)
                if live(3, lo, hi):
                    low_a(it - 3, 0, lo)
                route(it, lo, hi, 12)
                if live(0, lo, hi):
                    dve.wait_ge(s_rs1, it + 1)
                    if lo > 0:
                        dve.wait_ge(s_tT, it)
                        dve.wait_ge(s_xa, it * 2)
                    for j in range(2):
                        xt = x_all[:, bass.ds(it * 2 + j, 1), :].rearrange("p a d -> p (a d)")
                        dve.tensor_scalar(tbuf[:, j, :], xt, mv1[:, j, 0:1], rs1[:, j:j + 1],
                                          ALU.subtract, ALU.mult).then_inc(s_t, 1)
                if live(1, lo, hi):
                    p = it - 1
                    dve.wait_ge(s_shi, p + 1)
                    dve.tensor_tensor(slo[:, :, :], st[:, :, :], shi[:, :, :].bitcast(F32),
                                      ALU.subtract).then_inc(s_slo, 1)
                if live(3, lo, hi):
                    product_a(it - 3, 1, lo)
                route(it, lo, hi, 13, 14, 15)
                if live(3, lo, hi):
                    finish_a(it - 3, 0, lo)
                route(it, lo, hi, 16)
                if live(3, lo, hi):
                    low_a(it - 3, 1, lo)
                route(it, lo, hi, 17, 18, 19)

            for it in range(4):
                body(it, it, it)
            for g in range(2, 4):
                dve.wait_ge(l_x[g], 16)
            with dve.Fori(4, NP) as it:
                body(it, 4, NP - 1)
            for it in range(NP, NP + 4):
                body(it, it, it)

            dve.wait_ge(s_rt, NP * KR)
            link(dve.tensor_tensor(nE[:, :], rbase[:, :], const("eoff"), ALU.subtract))
            b3 = big3[:, 0:E * NT].rearrange("p (e t) -> p e t", e=E)
            link(dve.tensor_tensor(b3, nE[:, :].unsqueeze(2).to_broadcast([P, E, NT]),
                                   const("thr").unsqueeze(1).to_broadcast([P, E, NT]), ALU.is_gt))
            link(dve.tensor_reduce(tl[:, :], b3, AX.X, ALU.add))
            link(dve.tensor_tensor_scan(cum[:, :], const("ones")[:, 0:E], tl[:, :], 0.0, ALU.mult, ALU.add))
            r0 = slice(0, 1)
            S, J = SMAX, E + 2
            one = const("ones")[r0, 0:E]
            tl0, cum0 = tl[r0, :], cum[r0, :]
            total = cum[r0, E - 1:E]
            link(dve.tensor_scalar(ne[:, :], tl0, 1.0, None, ALU.min))
            link(dve.tensor_copy(ne[:, 0:1], one[:, 0:1]))
            link(dve.tensor_scalar(rmt[:, :], tl0, -float(P), float(R), ALU.mult, ALU.add))
            link(dve.tensor_tensor_scan(ordn[:, :], one, ne[:, :], 0.0, ALU.mult, ALU.add))
            steps_c = const("steps")[r0, :]

            def over(v, n):
                return v[r0, :].unsqueeze(1).to_broadcast([1, n, E])

            def per(c, n):
                return c.unsqueeze(2).to_broadcast([1, n, E])

            ge = big3[r0, 0:S * E].rearrange("o (s e) -> o s e", e=E)
            state = st[:, :, :].rearrange("p a b -> p (a b)")
            tmp3 = state[r0, 0:S * E].rearrange("o (s e) -> o s e", e=E)
            link(dve.tensor_tensor(ge, per(steps_c, S), over(cum, S), ALU.is_ge))
            link(dve.tensor_tensor(tmp3, ge, over(ne, S), ALU.mult))
            link(dve.tensor_reduce(tq[:, 0:S], tmp3, AX.X, ALU.add))
            link(dve.tensor_copy(tq[:, S:S + 1], ordn[:, E - 1:E]))
            link(dve.tensor_scalar(tf[:, TB_NEED:TB_NEED + S], tq[:, 0:S], 2.0, None, ALU.add))
            link(dve.tensor_scalar(tqi[:, :], tq[:, :], 1.0, None, ALU.add))
            link(dve.tensor_scalar(tqi[:, :], tqi[:, :], 1, None, ALU.bitwise_and))
            link(dve.tensor_scalar(tf[:, TB_OFF:TB_OFF + S], tqi[:, 0:S], float(WSZ), None, ALU.mult))
            link(dve.tensor_scalar(tf[:, TB_COFF:TB_COFF + 1], tqi[:, S:S + 1], float(WSZ), None, ALU.mult))
            link(dve.tensor_scalar(tf[:, TB_CNEED:TB_CNEED + 1], ordn[:, E - 1:E], 2.0, None, ALU.add))
            link(dve.tensor_scalar(tf[:, TB_JEND:TB_JEND + 1], ordn[:, E - 1:E], 2.0, None, ALU.add))
            link(dve.tensor_tensor(tmp3, ge, over(rmt, S), ALU.mult))
            link(dve.tensor_reduce(tq[:, 0:S], tmp3, AX.X, ALU.add))
            link(dve.scalar_tensor_tensor(tf[:, TB_ROW:TB_ROW + S], steps_c, float(P), tq[:, 0:S],
                                          ALU.mult, ALU.add))
            link(dve.tensor_copy(tf[:, TB_N:TB_N + E], nE[r0, :]))
            o3 = big3[r0, 0:J * E].rearrange("o (s e) -> o s e", e=E)
            link(dve.tensor_tensor(o3, over(ordn, J), per(const("jseq")[r0, :], J), ALU.is_lt))
            link(dve.tensor_reduce(tf[:, TB_ORDER:TB_ORDER + J], o3, AX.X, ALU.add))
            link(dve.tensor_tensor(o3, over(ordn, J), per(const("jseq0")[r0, :], J), ALU.is_le))
            link(dve.tensor_tensor(o3, o3, over(tl, J), ALU.mult))
            link(dve.tensor_reduce(tf[:, TB_FIN:TB_FIN + J], o3, AX.X, ALU.add))
            ev = big3[r0, 0:S // 2]
            link(dve.tensor_scalar(ev, const("even")[r0, :], total, None, ALU.is_lt))
            link(dve.tensor_reduce(tq[:, 0:1], ev, AX.X, ALU.add))
            link(dve.tensor_scalar(tf[:, TB_ITERS:TB_ITERS + 1], tq[:, 0:1], -2.0, None, ALU.add))
            link(dve.tensor_copy(tf[:, TB_PAR:TB_PAR + J + 2], const("par")[r0, :]))
            dve.tensor_copy(ti[:, :], tf[:, :]).then_inc(s_tab, 1)

            def routed():
                ty = state[:, 0:NT * E].rearrange("p (t e) -> p t e", e=E)
                yp = state[:, NT * E:NT * E + NT]
                link(dve.tensor_tensor(base[:, :], cum[:, :], tl[:, :], ALU.subtract))
                link(dve.scalar_tensor_tensor(base[:, :], base[:, :], float(P), const("eoff"),
                                              ALU.mult, ALU.subtract))
                for k in range(2):
                    link(dve.tensor_tensor(ty, oh[k][:, :, :], sc[:, :, :], ALU.mult))
                    link(dve.tensor_reduce(sw[:, k, :], ty, AX.X, ALU.add))
                    link(dve.tensor_tensor(ty, oh[k][:, :, :], base[:, :].unsqueeze(1).to_broadcast([P, NT, E]),
                                           ALU.mult))
                    link(dve.tensor_reduce(yp, ty, AX.X, ALU.add))
                    link(dve.tensor_tensor(pos[:, :, k], pos[:, :, k], yp, ALU.add))
                link(dve.tensor_tensor(den[:, :], sw[:, 0, :], sw[:, 1, :], ALU.add))
                link(dve.tensor_scalar(den[:, :], den[:, :], 1e-12, None, ALU.max))
                link(dve.reciprocal(den[:, :], den[:, :]))
                for k in range(2):
                    link(dve.tensor_tensor(wts[:, :, k], sw[:, k, :], den[:, :], ALU.mult))

            def lows(sec, i, j):
                dve.wait_ge(q[sec, "xhi"], i * 2 + (j + 1))
                dve.tensor_tensor(xbl[:, j, :], bank[j][:, :], xbh[:, j, :].bitcast(F32),
                                  ALU.subtract).then_inc(q[sec, "xlo"], 1)

            def offsets(sec, i, j, first):
                if not first:
                    dve.wait_ge(s_gath[j], i * 32)
                for k in range(2):
                    dve.tensor_copy(idx[j][k][:, :], pos[:, bass.ds(i * 2 + j, 1), k]).then_inc(q[sec, "idx"], 1)

            def finish(sec, i, j, first):
                dve.wait_ge(q[sec, "dn"], i * 2 + (j + 1))
                xt = x_all[:, bass.ds(i * 2 + j, 1), :].rearrange("p a d -> p (a d)")
                if sec == "C":
                    y, n = ybuf[:, j, :], i * 2 + (j + 1)
                    dve.wait_ge(s_gath[j], i * 32 + 32)
                    if not first:
                        dve.wait_ge(q["C", "ydma"][j], i * 16)
                    w = [wts[:, bass.ds(i * 2 + j, 1), k] for k in range(2)]
                    dve.scalar_tensor_tensor(y, tbuf[:, j, :], w[0], bank[5 + j][:, :],
                                             ALU.mult, ALU.add).then_inc(q["C", "y"], 1)
                    dve.wait_ge(q["C", "y"], n)
                    dve.scalar_tensor_tensor(y, xtf[:, j, :], w[1], y, ALU.mult, ALU.add).then_inc(s_c2, 1)
                    dve.wait_ge(s_c2, n)
                    dve.tensor_tensor(y, y, mods[:, 5, :], ALU.mult).then_inc(s_c3, 1)
                    dve.wait_ge(s_c3, n)
                    dve.tensor_tensor(y, y, xt, ALU.add).then_inc(s_c4, 1)

            def section(sec):
                def step(i, j, first, last):
                    if sec == "C" and not first and not last:
                        offsets("C", i + j, 1 - j, False)
                    if not last:
                        if not first:
                            dve.wait_ge(q[sec, "up"], i * 2 + j)
                        lows(sec, i + j, 1 - j)
                    dve.wait_ge(q[sec, "silu"], i * 2 + (j + 1))
                    dve.wait_ge(q[sec, "up"], i * 2 + (j + 1))
                    if not first:
                        dve.wait_ge(q[sec, "gt"], i * 2 + j)
                    dve.tensor_tensor(gbuf[:, 0:F], s1[:, :], bank[3][:, 0:F], ALU.mult).then_inc(q[sec, "g"], 1)
                    dve.wait_ge(q[sec, "ghi"], i * 2 + (j + 1))
                    if not first:
                        dve.wait_ge(q[sec, "dn"], i * 2 + j)
                    dve.tensor_tensor(gtl[:, :], bank[4][:, 0:FP], gth[:, :].bitcast(F32),
                                      ALU.subtract).then_inc(q[sec, "glo"], 1)
                    if not first and sec != "B":
                        finish(sec, i - 1 + j, 1 - j, isinstance(i, int) and i <= 1 - j)
                return step

            dve.wait_ge(s_stp, NP)
            dve.wait_ge(s_at, NP)
            dve.wait_ge(s_tab, 1)
            iters = pairs_of_b(dve)
            lows("B", 0, 0)
            routed()
            steps(dve, iters, section("B"))
            dve.wait_ge(s_fa, NT)
            for j in range(2):
                dve.wait_ge(q["B", "ydma"][j], iters * 16)
            for j in range(2):
                offsets("C", 0, j, True)
            lows("C", 0, 0)
            steps(dve, NP, section("C"))
            finish("C", NP - 1, 1, False)


def kernel(L0_attn_x, L0_attn_B, L0_attn_C, L0_attn_D, L0_ffn_gate_w, L0_ffn_router_bias, L0_ffn_W1,
           L0_ffn_W3, L0_ffn_W2, L0_ffn_sw1, L0_ffn_sw3, L0_ffn_sw2, L0_c, L0_wmod):
    import numpy as np
    import concourse.bacc as bacc
    from concourse.bass_utils import run_bass_kernel_spmd

    f = np.float32

    def chunks(a):
        return a.reshape(-1, P, a.shape[1]).transpose(1, 0, 2)

    packed = np.zeros((E + 2, P, WSZ), f)

    def pack(n, w1, w3, w2):
        packed[n, :, :WDN] = np.concatenate([chunks(w1), chunks(w3)], axis=2).reshape(P, WDN)
        w2p = np.zeros((FP, D), f)
        w2p[:F] = w2
        packed[n, :, WDN:] = chunks(w2p).reshape(P, KF * D)

    W1, W3, W2 = (np.asarray(a) for a in (L0_ffn_W1, L0_ffn_W3, L0_ffn_W2))
    s1, s3, s2 = (np.asarray(a) for a in (L0_ffn_sw1, L0_ffn_sw3, L0_ffn_sw2))
    for e in range(E):
        pack(e, W1[e], W3[e], W2[e])
    for n, h in ((SHARED_A, slice(0, F)), (SHARED_B, slice(F, 2 * F))):
        pack(n, s1[h].T, s3[h].T, s2[:, h].T)

    const = np.zeros((P, CW), f)

    def put(name, v):
        const[:, COL[name][0]:COL[name][1]] = v

    put("ident", np.eye(P))
    put("tri", np.triu(np.ones((P, P)), 1))
    put("ones", 1.0)
    put("io", np.tile(np.arange(E), 2))
    put("io8", np.tile(np.arange(E) + E, 2))
    put("eoff", np.arange(E) * R)
    put("steps", np.arange(SMAX))
    put("thr", np.arange(NT) * P)
    put("even", np.arange(SMAX // 2) * 2)
    put("jseq", np.arange(E + 2) + 1)
    put("jseq0", np.arange(E + 2))
    put("par", np.arange(E + 4) % 2 * WSZ)

    arrays = {
        "x": np.asarray(L0_attn_x)[0],
        "ccol": np.asarray(L0_c).reshape(KD, P).T,
        "wmod": np.asarray(L0_wmod),
        "bt": chunks(np.asarray(L0_attn_B).T),
        "ct": chunks(np.asarray(L0_attn_C).T),
        "dvec": np.asarray(L0_attn_D)[None, :],
        "gwt": chunks(np.asarray(L0_ffn_gate_w).T),
        "rb": np.asarray(L0_ffn_router_bias)[None, :],
        "w_all": packed.reshape((E + 2) * P, WSZ),
        "consts": const,
    }
    arrays = {k: np.ascontiguousarray(a) for k, a in arrays.items()}
    nc = bacc.Bacc("TRN2", target_bir_lowering=False, num_devices=1)
    args = [nc.dram_tensor(k, a.shape, mybir.dt.from_np(a.dtype), kind="ExternalInput").ap()
            for k, a in arrays.items()]
    res = nc.dram_tensor("out", (T, D), F32, kind="ExternalOutput").ap()
    build(nc, *args, res)
    r = run_bass_kernel_spmd(nc, [arrays], core_ids=[0])
    return r.results[0]["out"].reshape(1, T, D)
```

```python
from contextlib import ExitStack

import concourse.bass as bass
from concourse import mybir

F32 = mybir.dt.float32
F32R = mybir.dt.float32r
BF16 = mybir.dt.bfloat16
I32 = mybir.dt.int32
U32 = mybir.dt.uint32
ALU = mybir.AluOpType
ACT = mybir.ActivationFunctionType
AX = mybir.AxisListType

P = 128
T, D, N, F, E = 2048, 512, 256, 352, 8
KD, KN = D // P, N // P
NT = T // P
NP = NT // 2
KF = -(-F // P)
FP = KF * P
UP = 2 * F
WSZ = KD * UP + KF * D
WDN = KD * UP
PIECES = [(0, WDN // 2), (WDN // 2, WDN), (WDN, WSZ)]
NW = len(PIECES)
SMAX = 2 * T // P + E
SMIN = 2 * T // P
R = T + P
PAD_ACT = 3
KR = 20
SHARED_A, SHARED_B = E + 1, E
EPS = 1e-5
BIG = 3.0e38

_sizes = [("ident", P), ("tri", P), ("ones", P), ("io", 2 * E), ("io8", 2 * E), ("eoff", E),
          ("steps", SMAX), ("thr", NT), ("even", SMAX // 2), ("jseq", E + 2), ("jseq0", E + 2),
          ("par", E + 4)]
COL, _at = {}, 0
for _n, _s in _sizes:
    COL[_n] = (_at, _at + _s)
    _at += _s
CW = _at

TB_ROW, TB_OFF = 0, SMAX
TB_NEED = TB_OFF + SMAX + 1
TB_ORDER = TB_NEED + SMAX + 1
TB_FIN = TB_ORDER + E + 2
TB_N = TB_FIN + E + 2
TB_ITERS = TB_N + E
TB_JEND = TB_ITERS + 1
TB_PAR = TB_ITERS + 2
TBW = TB_PAR + E + 4


def build(nc, x, ccol, wmod, bt, ct, dvec, gwt, rb, w_all, consts, out):
    hs = nc.dram_tensor("hs_rows", (T, D), F32, kind="Internal").ap()
    xs = nc.dram_tensor("xs_rows", (E * R + P, D), F32, kind="Internal").ap()
    ys = nc.dram_tensor("ys_rows", (SMAX * P, D), F32, kind="Internal").ap()

    with ExitStack() as ctx:
        def sb(name, shape, dt=F32):
            return ctx.enter_context(nc.sbuf_tensor(name, shape, dt))

        def sem(name):
            return ctx.enter_context(nc.semaphore(name))

        bank = [ctx.enter_context(nc.psum_tensor(f"bank{i}", [P, 512], F32)) for i in range(8)]

        cst = sb("cst", [P, CW])

        def const(name):
            return cst[:, COL[name][0]:COL[name][1]]

        ident = const("ident")
        tri_b = sb("tri_b", [P, P], BF16)
        ones_b = sb("ones_b", [P, P], BF16)
        x_all = sb("x_all", [P, NT, D])
        whi = sb("whi", [P, 2 * WSZ], F32R)
        wlo = sb("wlo", [P, 2 * WSZ], F32R)
        raw = sb("raw", [P, WSZ])
        mods = sb("mods", [P, 6, D])
        a12 = sb("a12", [P, 2, D])
        bhi = sb("bhi", [P, KD, N], F32R)
        blo = sb("blo", [P, KD, N], F32R)
        chi = sb("chi", [P, KN, D], F32R)
        clo = sb("clo", [P, KN, D], F32R)
        gw = sb("gw", [P, KD, E])
        rbias = sb("rbias", [P, E])
        cols = sb("cols", [P, 2, KD])
        bsa = sb("bsa", [P, KN])
        c_in = sb("c_in", [P, KD])
        sil = sb("sil", [P, KD])
        eps_t = sb("eps_t", [P, 2])
        mhalf = sb("mhalf", [P, 2])
        zrow = sb("zrow", [P, D])
        tbuf = sb("tbuf", [P, 2, D])
        tmpa = sb("tmpa", [P, 2, D])
        h2 = sb("h2", [P, 2, D])
        thi = sb("thi", [P, KD, 2 * P], F32R)
        tlo = sb("tlo", [P, KD, 2 * P], F32R)
        st = sb("st", [P, KN, 2 * P])
        shi = sb("shi", [P, KN, 2 * P], F32R)
        slo = sb("slo", [P, KN, 2 * P], F32R)
        xtf = sb("xtf", [P, 2, D])
        bn1 = sb("bn1", [P, 2, 6])
        bn2 = sb("bn2", [P, 2, 6])
        mv1 = sb("mv1", [P, 2, 2])
        mv2 = sb("mv2", [P, 2, 2])
        ve1 = sb("ve1", [P, 2])
        ve2 = sb("ve2", [P, 2])
        rs1 = sb("rs1", [P, 2])
        rs2 = sb("rs2", [P, 2])
        sc = sb("sc", [P, NT, E])
        oh = [sb("oh1", [P, NT, E]), sb("oh2", [P, NT, E])]
        sel = sb("sel", [P, 2, E])
        ra = sb("ra", [P, 2, E])
        rc = sb("rc", [P, 2, E])
        rm = sb("rm", [P, 2])
        ri = sb("ri", [P, 2])
        mask = sb("mask", [P, 2, E], BF16)
        rbase = sb("rbase", [P, E])
        idx4 = [sb(f"idx4{b}", [P, 4], U32) for b in range(2)]
        sw = sb("sw", [P, 2, NT])
        den = sb("den", [P, NT])
        wts = sb("wts", [P, NT, 2])
        pos = sb("pos", [P, NT, 2])
        nE = sb("nE", [P, E])
        idx = [[sb(f"idx{j}{k}", [P, 1], U32) for k in range(2)] for j in range(2)]
        tr = sb("tr", [1, SMAX])
        ev = sb("ev", [1, SMAX // 2])
        ti = sb("ti", [1, TBW], I32)
        tl = sb("tl", [P, E])
        cum = sb("cum", [P, E])
        base = sb("base", [P, E])
        ne = sb("ne", [1, E])
        rmt = sb("rmt", [1, E])
        ordn = sb("ordn", [1, E])
        tq = sb("tq", [1, SMAX + 1])
        tqi = sb("tqi", [1, SMAX + 1], I32)
        xah, xal = sb("xah", [P, 2, D], F32R), sb("xal", [P, 2, D], F32R)
        xbh = thi[:, :, :].rearrange("p a b -> p (a b)").rearrange("p (b d) -> p b d", b=2)
        xbl = tlo[:, :, :].rearrange("p a b -> p (a b)").rearrange("p (b d) -> p b d", b=2)
        s1 = sb("s1", [P, F])
        gbuf = sb("gbuf", [P, FP])
        gth, gtl = sb("gth", [P, FP], F32R), sb("gtl", [P, FP], F32R)
        big3 = sb("big3", [P, SMAX * E + 8])
        xin = h2
        ybuf = tmpa
        hrow = [mods[:, 0:2, :], tmpa[:, :, :]]
        fbuf = mods[:, 2, :]
        btr = xtf[:, :, :].rearrange("p b d -> p (b d)").rearrange("p (k n) -> p k n", k=KD)
        cga = h2
        dbc = st[:, :, :].rearrange("p k n -> p (k n)")
        silb = [gbuf[:, k * P:(k + 1) * P] for k in range(KF)] + [big3[:, 0:P]]
        ring = [x_all[:, NT // 2 + r * KD:NT // 2 + (r + 1) * KD, :] for r in range(2)] + [
            raw[:, r * KD * D:(r + 1) * KD * D].rearrange("p (k n) -> p k n", k=KD) for r in range(2)]

        l_small = sem("l_small")
        l_gate = sem("l_gate")
        l_attn = sem("l_attn")
        l_x = [sem(f"l_x{g}") for g in range(4)]
        l_wm = [sem(f"l_wm{j}") for j in range(4)]
        l_w0 = [sem(f"l_w0{k}") for k in range(NW)]
        s_w0 = sem("s_w0")
        s_sil = sem("s_sil")
        s_silb = sem("s_silb")
        s_mod = sem("s_mod")
        s_modc = sem("s_modc")
        s_colT = sem("s_colT")
        s_cols = sem("s_cols")
        s_bsaT = sem("s_bsaT")
        s_ga, s_gb = sem("s_ga"), sem("s_gb")
        s_cga = sem("s_cga")
        s_bhi = sem("s_bhi")
        s_fold = sem("s_fold")
        s_foldc = sem("s_foldc")
        s_a12 = sem("s_a12")
        chain = sem("chain")
        pchain = sem("pchain")
        s_bn1, s_st1, s_rs1, s_ve1 = sem("s_bn1"), sem("s_st1"), sem("s_rs1"), sem("s_ve1")
        s_bn2, s_st2, s_rs2, s_ve2 = sem("s_bn2"), sem("s_st2"), sem("s_rs2"), sem("s_ve2")
        s_t = sem("s_t")
        s_tT = sem("s_tT")
        s_thi = sem("s_thi")
        s_tlo = sem("s_tlo")
        s_stp = sem("s_stp")
        s_tanh = sem("s_tanh")
        s_shi = sem("s_shi")
        s_slo = sem("s_slo")
        s_xa, s_xb, s_xd = sem("s_xa"), sem("s_xb"), sem("s_xd")
        s_at = sem("s_at")
        s_x1 = sem("s_x1")
        s_u = sem("s_u")
        s_h2 = sem("s_h2")
        s_nat = sem("s_nat")
        s_h2T = sem("s_h2T")
        s_xtf = sem("s_xtf")
        s_gate = sem("s_gate")
        s_sc = sem("s_sc")
        s_rt = sem("s_rt")
        s_hrow = [sem("s_hrow"), sem("s_hrow_last")]
        s_fa = sem("s_fa")
        s_scat = sem("s_scat")
        s_rank = sem("s_rank")
        s_cnt, s_row, s_tab = sem("s_cnt"), sem("s_row"), sem("s_tab")
        s_pad, s_pad_act = sem("s_pad"), sem("s_pad_act")
        w_hi, w_raw, w_ready = [sem(f"w_hi{k}") for k in range(NW)], sem("w_raw"), sem("w_ready")
        q = {}
        for sec in "ASC":
            for n in ("xt", "xhi", "xlo", "up", "silu", "g", "gt", "ghi", "glo", "dn", "y", "idx"):
                q[sec, n] = sem(f"{n}_{sec}")
            q[sec, "xin"] = [sem(f"xin{j}_{sec}") for j in range(2)]
            q[sec, "ydma"] = [sem(f"ydma{j}_{sec}") for j in range(2)]
        s_gath = [sem(f"s_gath{j}") for j in range(2)]
        s_c2, s_c3, s_c4 = sem("s_c2"), sem("s_c3"), sem("s_c4")

        block = ctx.enter_context(nc.Block())
        WM = [1, 0, 2, 4, 3, 5]

        def iterations(eng, body, first=0):
            for it in range(first, 5):
                body(it, it, it)
            with eng.Fori(5, NP) as it:
                body(it, 5, NP - 1)
            for it in range(NP, NP + 4):
                body(it, it, it)

        at = [0]

        def value(eng, v):
            if isinstance(v, int):
                return v
            at[0] += 1
            reg = eng.alloc_register(f"value{at[0]}")
            eng.reg_mov(reg, v)
            return reg

        def pairs_of_b(eng):
            return eng.value_load(ti[0:1, TB_ITERS:TB_ITERS + 1], min_val=NP - 2, max_val=SMAX // 2 - 2) + 2

        def is_last(lo):
            return int(lo == NP + 2)

        def live(lag, lo, hi):
            return lo - lag >= 0 and hi - lag < NP

        def pad(eng, first, end, done):
            eng.wait_ge(s_cnt, 1)
            for e in range(first, end):
                n = eng.value_load(ti[0:1, TB_N + e:TB_N + e + 1], min_val=0, max_val=T)
                eng.dma_start(xs[bass.ds(n + e * R, P), :], zrow[:, :]).then_inc(done, 16)

        def steps(eng, iters, step):
            for i in range(2):
                for j in range(2):
                    step(i, j, None, i + j == 0)
            with eng.Fori(2, iters) as i:
                for j in range(2):
                    step(i, j, None, False)
            for c in range(2):
                for j in range(2):
                    step(iters + c, j, c, False)
            with eng.Fori(2, NP - 1) as c:
                for j in range(2):
                    step(iters + c, j, c, False)
            for j in range(2):
                step(iters + (NP - 1), j, NP - 1, j == 1)

        @block.sync
        def _(sp):
            wm_v = wmod.rearrange("(k p) (j n) -> j p k n", p=P, j=6)
            x_v = x.rearrange("(g b p) d -> g p b d", b=4, p=P)

            def piece(i):
                if i >= 4:
                    sp.wait_ge(s_mod, i - 3)
                sp.dma_start(ring[i % 4], wm_v[WM[i]]).then_inc(l_wm[i % 4], 16)

            def tiles(g):
                sp.dma_start(x_all[:, 4 * g:4 * g + 4, :], x_v[g]).then_inc(l_x[g], 16)

            sp.dma_start(c_in[:, :], ccol).then_inc(l_small, 16)
            sp.dma_start(cst[:, :], consts).then_inc(l_small, 16)
            piece(0)
            piece(1)
            tiles(0)
            piece(2)
            sp.dma_start(btr, bt).then_inc(l_attn, 16)
            sp.dma_start(dbc, dvec.to_broadcast([P, D])).then_inc(l_attn, 16)
            sp.dma_start(cga[:, :, :], ct).then_inc(l_attn, 16)
            for i in range(3, 6):
                piece(i)
            sp.wait_ge(s_mod, 4)
            for k, (a, b) in enumerate(PIECES):
                sp.dma_start(raw[:, a:b], w_all[SHARED_A * P:(SHARED_A + 1) * P, a:b]).then_inc(l_w0[k], 16)
            tiles(1)
            sp.dma_start(gw[:, :, :], gwt).then_inc(l_gate, 16)
            sp.dma_start(rbias[:, :], rb.to_broadcast([P, E])).then_inc(l_gate, 16)
            sp.wait_ge(pchain, 3)
            sp.dma_start(ys[SMIN * P:, :].rearrange("(s p) d -> p s d", p=P),
                         zrow[:, :].unsqueeze(1).to_broadcast([P, SMAX - SMIN, D])).then_inc(s_pad, 16)
            sp.dma_start(xs[E * R:, :], zrow[:, :]).then_inc(s_pad, 16)
            sp.wait_ge(s_mod, 6)
            for g in range(2, 4):
                tiles(g)

            def body(it, lo, hi):
                if live(3, lo, hi):
                    p = it - 3
                    left = value(sp, p * 64)
                    sp.wait_ge(s_nat, p * 16 + 16)
                    if is_last(lo):
                        sp.wait_ge(s_xd, NP)
                    elif lo > 3:
                        sp.wait_ge(s_scat, left)
                    sp.dma_start(hrow[is_last(lo)], hs[bass.ds(p * 2 * P, 2 * P), :].rearrange("(b p) d -> p b d", p=P)
                                 ).then_inc(s_hrow[is_last(lo)], 16)
                if live(2, lo, hi):
                    p = it - 2
                    sp.wait_ge(s_h2, p * 2 + 2)
                    sp.dma_start(hs[bass.ds(p * 2 * P, 2 * P), :].rearrange("(b p) d -> p b d", p=P),
                                 h2[:, :, :]).then_inc(s_nat, 16)

            sp.wait_ge(s_a12, 3)
            sp.wait_ge(s_colT, 1)
            iterations(sp, body)

            def load(src, j, row):
                sp.dma_start(xin[:, j, :], src[bass.ds(row, P), :]).then_inc(q["S", "xin"][j], 16)

            pad(sp, 0, E - PAD_ACT, s_pad)
            sp.wait_ge(s_pad, 16 * (E - PAD_ACT + 2))
            sp.wait_ge(s_pad_act, 16 * PAD_ACT)
            sp.wait_ge(s_scat, 64 * NP)
            sp.wait_ge(s_row, 1)

            def row_of(n):
                return sp.value_load(ti[0:1, bass.ds(n + TB_ROW, 1)], min_val=0, max_val=E * R)

            sp.wait_ge(s_h2T, NP)
            for j in range(2):
                load(xs, j, row_of(j))
            sp.wait_ge(s_tab, 1)
            iters = pairs_of_b(sp)

            def next_b(i, j):
                row = row_of(i * 2 + (j + 3))
                sp.wait_ge(q["S", "xt"], i * 2 + (j + 2))
                load(xs, 1 - j, row)

            def next_c(i, j, tile):
                sp.wait_ge(q["S", "xt"], i * 2 + (j + 2))
                load(hs, 1 - j, tile * P)

            def store_y(i, j):
                sp.wait_ge(q["S", "y"], i * 2 + (j + 1))
                sp.dma_start(ys[bass.ds(i * (2 * P) + j * P, P), :], ybuf[:, j, :]).then_inc(q["S", "ydma"][j], 16)

            def store_out(c, j):
                sp.wait_ge(s_c4, c * 2 + (j + 1))
                sp.dma_start(out[bass.ds(c * (2 * P) + j * P, P), :], ybuf[:, j, :]).then_inc(q["C", "ydma"][j], 16)

            sp.wait_ge(q["S", "xt"], 1)
            load(xs, 0, row_of(2))
            next_b(0, 0)
            next_b(0, 1)
            store_y(0, 0)
            with sp.Fori(1, iters - 2) as i:
                for j in range(2):
                    next_b(i, j)
                    store_y(i - 1 + j, 1 - j)
            next_b(iters - 2, 0)
            store_y(iters - 3, 1)
            for n in range(-3, 0):
                j = n % 2
                next_c(iters + (n - j) // 2, j, n + 3)
                store_y(iters + (n - j) // 2 - 1 + j, 1 - j)
            next_c(iters, 0, 3)
            store_y(iters - 1, 1)
            next_c(iters, 1, 4)
            store_out(0, 0)
            with sp.Fori(1, NP - 2) as c:
                for j in range(2):
                    next_c(iters + c, j, c * 2 + (j + 3))
                    store_out(c - 1 + j, 1 - j)
            next_c(iters + (NP - 2), 0, NT - 1)
            store_out(NP - 3, 1)
            for c in (NP - 2, NP - 1):
                for j in range(2):
                    store_out(c, j)
            for j in range(2):
                sp.wait_ge(q["C", "ydma"][j], 16 * NP)

        @block.gpsimd
        def _(pool):
            pool.memset(eps_t[:, :], EPS).then_inc(pchain, 1)
            pool.memset(mhalf[:, :], -0.5).then_inc(pchain, 1)
            pool.memset(zrow[:, :], 0.0).then_inc(pchain, 1)
            pool.wait_ge(pchain, 3)

            def fetch(row, off, slot_free):
                pool.dma_start(raw[:, :], w_all[bass.ds(row * P, P), :]).then_inc(w_raw, 16)
                slot_free()
                for k, (a, b) in enumerate(PIECES):
                    pool.dma_start(whi[:, bass.ds(off + a, b - a)], w_all[bass.ds(row * P, P), a:b],
                                   max_dma_last_dim=8192).then_inc(w_hi[k], 16)

            def low(n, off, pieces=range(NW)):
                raw_there, hi_there = value(pool, n * 16), value(pool, n * 16)
                for k in pieces:
                    a, b = PIECES[k]
                    pool.wait_ge(pchain, 3)
                    if k == 0:
                        pool.wait_ge(w_raw, raw_there)
                    pool.wait_ge(w_hi[k], hi_there)
                    pool.tensor_tensor(wlo[:, bass.ds(off + a, b - a)], raw[:, a:b],
                                       whi[:, bass.ds(off + a, b - a)].bitcast(F32), ALU.subtract).then_inc(w_ready, 1)

            def with_d(it, lo, hi):
                if live(1, lo, hi):
                    p = it - 1
                    pool.wait_ge(s_t, p * 2 + 2)
                    if lo > 1:
                        pool.wait_ge(s_xd, p)
                    for j in range(2):
                        pool.tensor_tensor(tmpa[:, j, :], tbuf[:, j, :], a12[:, 0, :], ALU.mult).then_inc(s_xa, 1)
                    pool.wait_ge(s_xa, p * 2 + 2)
                    for j in range(2):
                        pool.tensor_tensor(tmpa[:, j, :], tmpa[:, j, :], a12[:, 1, :], ALU.add).then_inc(s_xb, 1)
                    pool.wait_ge(s_xb, p * 2 + 2)
                    xp = x_all[:, bass.ds(p * 2, 2), :]
                    pool.tensor_tensor(xp, xp, tmpa[:, :, :], ALU.add).then_inc(s_xd, 1)

            def body(it, lo, hi):
                if lo > 1:
                    with_d(it, lo, hi)
                if live(2, lo, hi):
                    p = it - 2
                    pool.wait_ge(s_st2, p * 2 + 2)
                    pool.tensor_tensor(ve2[:, :], mv2[:, :, 1], eps_t[:, :], ALU.add).then_inc(s_ve2, 1)
                    pool.wait_ge(s_ve2, p + 1)
                    if lo > 2:
                        pool.wait_ge(s_h2, p * 2)
                    pool.tensor_tensor(rs2[:, :], ve2[:, :], mhalf[:, :], ALU.pow).then_inc(s_rs2, 1)
                if live(0, lo, hi):
                    pool.wait_ge(s_st1, it * 2 + 2)
                    pool.tensor_tensor(ve1[:, :], mv1[:, :, 1], eps_t[:, :], ALU.add).then_inc(s_ve1, 1)
                    pool.wait_ge(s_ve1, it + 1)
                    if lo > 0:
                        pool.wait_ge(s_t, it * 2)
                    pool.tensor_tensor(rs1[:, :], ve1[:, :], mhalf[:, :], ALU.pow).then_inc(s_rs1, 1)
                if lo == 1:
                    with_d(it, lo, hi)
                if lo == hi == 3:
                    pool.wait_ge(w_ready, NW)
                    fetch(0, WSZ, lambda: None)

                def scatter():
                    p = it - 3
                    landed, known = value(pool, p * 16 + 16), value(pool, p * KR + KR)
                    pool.wait_ge(s_fold, 1)
                    pool.wait_ge(s_hrow[is_last(lo)], 16 if is_last(lo) else landed)
                    pool.wait_ge(s_rt, known)
                    for j in range(2):
                        for k in range(2):
                            pool.indirect_dma_start(
                                xs[:, :], bass.IndirectOffsetOnAxis(ap=idx4[is_last(lo)][:, 2 * j + k:2 * j + k + 1],
                                                              axis=0),
                                hrow[is_last(lo)][:, j, :], None).then_inc(s_scat, 16)

                def add_shared(p, j):
                    pool.wait_ge(q["A", "y"], p * 2 + (j + 1))
                    xt = x_all[:, bass.ds(p * 2 + j, 1), :].rearrange("p a d -> p (a d)")
                    pool.tensor_tensor(xt, xt, fbuf, ALU.add).then_inc(s_fa, 1)

                if live(4, lo, hi):
                    add_shared(it - 4, 1)
                if live(3, lo, hi) and is_last(lo):
                    scatter()
                if live(3, lo, hi):
                    add_shared(it - 3, 0)
                if live(3, lo, hi) and not is_last(lo):
                    scatter()
                if lo in (NP, NP + 1):
                    low(1, WSZ, [[0, 1], [2]][lo - NP])

            body(0, 0, 0)
            pool.wait_ge(s_ga, 1)
            pool.wait_ge(l_attn, 48)
            for n in range(KN):
                pool.tensor_tensor(cga[:, n, :], cga[:, n, :], mods[:, 2, :], ALU.mult).then_inc(s_cga, 1)
            pool.tensor_tensor(a12[:, 0, :], dbc, mods[:, 2, :], ALU.mult).then_inc(s_a12, 1)
            pool.wait_ge(s_a12, 1)
            pool.tensor_tensor(a12[:, 1, :], a12[:, 0, :], mods[:, 0, :], ALU.mult).then_inc(s_a12, 1)
            pool.wait_ge(s_a12, 2)
            pool.tensor_tensor(a12[:, 0, :], a12[:, 0, :], mods[:, 1, :], ALU.mult).then_inc(s_a12, 1)
            pool.wait_ge(s_a12, 3)
            iterations(pool, body, 1)

            def table(at, low_, high_):
                return pool.value_load(ti[0:1, bass.ds(at, 1)], min_val=low_, max_val=high_)

            pool.wait_ge(s_tab, 1)
            for j in range(2):
                pool.wait_ge(q["S", "xin"][j], 16)
            jend = table(TB_JEND, 3, E + 2)
            pool.wait_ge(w_ready, 2 * NW)
            fetch(table(TB_ORDER + 1, 0, E), 0, lambda: pool.wait_ge(q["A", "dn"], NT))
            low(2, 0)
            with pool.Fori(3, jend) as n:
                row = table(n + (TB_ORDER - 1), 0, E)
                fin = table(n + (TB_FIN - 2), 1, SMAX)
                off = table(n + (TB_PAR), 0, WSZ)
                pool.wait_ge(w_ready, n * NW)
                fetch(row, off, lambda: pool.wait_ge(q["S", "dn"], fin))
                low(n, off)
            iters = pairs_of_b(pool)
            stored = value(pool, iters * 16)
            pool.wait_ge(s_tab, 1)
            for j in range(2):
                pool.wait_ge(q["S", "ydma"][j], stored)

            def gather(i, j, first):
                known, used = value(pool, i * 4 + (2 * j + 2)), None if first else value(pool, i * 2 + (j - 1))
                pool.wait_ge(s_tab, 1)
                pool.wait_ge(q["C", "idx"], known)
                if not first:
                    pool.wait_ge(s_c2, used)
                for k, dst in ((0, tbuf), (1, xtf)):
                    pool.indirect_dma_start(dst[:, j, :], None, ys[:, :],
                                            bass.IndirectOffsetOnAxis(ap=idx[j][k][:, :], axis=0)
                                            ).then_inc(s_gath[j], 16)

            for j in range(2):
                gather(0, j, True)
            with pool.Fori(1, NP) as i:
                for j in range(2):
                    gather(i, j, False)

        @block.scalar
        def _(act):
            def hidden(p, j, lo):
                n = p * 2 + (j + 1)
                act.wait_ge(q["A", "up"], n)
                if lo > 3 or j:
                    act.wait_ge(q["A", "g"], p * 2 + j)
                act.activation(s1[:, :], bank[2][:, 0:F], ACT.Silu).then_inc(q["A", "silu"], 1)
                act.wait_ge(q["A", "gt"], n)
                if lo > 3 or j:
                    act.wait_ge(q["A", "dn"], p * 2 + j)
                act.activation(gth[:, :], bank[4 + j][:, 0:FP], ACT.Copy).then_inc(q["A", "ghi"], 1)

            def first_weights(k):
                a, b = PIECES[k]
                act.wait_ge(l_w0[k], 16)
                act.activation(whi[:, a:b], raw[:, a:b], ACT.Copy).then_inc(s_w0, 1)

            def body(it, lo, hi):
                if live(1, lo, hi):
                    p = it - 1
                    act.wait_ge(s_tT, p + 1)
                    if lo > 1:
                        act.wait_ge(s_stp, p)
                    for j in range(2):
                        act.activation(thi[:, :, j * P:j * P + P],
                                       bank[2 + j][:, :].rearrange("p (k m) -> p k m", k=KD),
                                       ACT.Copy).then_inc(s_thi, 1)
                    if lo == 1:
                        first_weights(0)
                        first_weights(1)
                if live(3, lo, hi):
                    p = it - 3
                    act.wait_ge(s_h2T, p + 1)
                    if lo > 3:
                        act.wait_ge(q["A", "up"], p * 2)
                        act.wait_ge(s_gate, p)
                    else:
                        act.wait_ge(s_gb, 1)
                    for j in range(2):
                        act.activation(xah[:, j, :], bank[4 + j][:, :], ACT.Copy).then_inc(q["A", "xhi"], 1)
                        act.activation(xtf[:, j, :], bank[4 + j][:, :], ACT.Copy).then_inc(s_xtf, 1)
                    act.wait_ge(s_gate, p + 1)
                    act.activation(sc[:, bass.ds(p * 2, 2), :],
                                   bank[7][:, 0:2 * E].rearrange("p (b e) -> p b e", b=2),
                                   ACT.Sigmoid).then_inc(s_sc, 1)
                    hidden(p, 0, lo)
                if live(1, lo, hi):
                    p = it - 1
                    act.wait_ge(s_stp, p + 1)
                    if lo > 1:
                        act.wait_ge(s_slo, p)
                    else:
                        act.wait_ge(s_fold, 1)
                        act.wait_ge(s_a12, 1)
                    for n in range(KN):
                        act.activation(st[:, n, :], bank[6][:, n * 2 * P:(n + 1) * 2 * P], ACT.Tanh,
                                       bias=bsa[:, n:n + 1]).then_inc(s_tanh, 1)
                    act.wait_ge(s_tanh, p * 2 + 2)
                    if lo > 1:
                        act.wait_ge(s_at, p)
                    act.activation(shi[:, :, :], st[:, :, :], ACT.Copy).then_inc(s_shi, 1)
                if is_last(lo):
                    pad(act, E - PAD_ACT, E, s_pad_act)
                if live(3, lo, hi):
                    hidden(it - 3, 1, lo)

            act.wait_ge(l_small, 32)
            act.activation(sil[:, :], c_in[:, :], ACT.Silu).then_inc(s_sil, 1)

            def modulation(i):
                m = WM[i]
                act.wait_ge(s_mod, i + 1)
                act.activation(mods[:, m, :], bank[i % 2][:, :], ACT.Identity,
                               bias=const("ones")[:, 0:1] if m in (1, 4) else zrow[:, 0:1]).then_inc(s_modc, 1)

            act.wait_ge(pchain, 3)
            for i in range(4):
                modulation(i)
            body(1, 1, 1)
            first_weights(2)
            modulation(4)
            body(2, 2, 2)
            modulation(5)
            iterations(act, body, 3)

            def high(i, j):
                act.wait_ge(q["S", "xt"], i * 2 + (j + 1))
                act.activation(xbh[:, j, :], bank[j][:, :], ACT.Copy).then_inc(q["S", "xhi"], 1)

            def result(i, j, first):
                act.wait_ge(q["S", "dn"], i * 2 + (j + 1))
                if not first:
                    act.wait_ge(q["S", "ydma"][j], i * 16)
                act.activation(ybuf[:, j, :], bank[5 + j][:, :], ACT.Copy).then_inc(q["S", "y"], 1)

            def step(i, j, c, end):
                first = isinstance(i, int) and end
                if first or not end:
                    if not first:
                        act.wait_ge(q["S", "up"], i * 2 + j)
                    high(i + j, 1 - j)
                act.wait_ge(q["S", "up"], i * 2 + (j + 1))
                if not first:
                    act.wait_ge(q["S", "g"], i * 2 + j)
                act.activation(s1[:, :], bank[2][:, 0:F], ACT.Silu).then_inc(q["S", "silu"], 1)
                act.wait_ge(q["S", "gt"], i * 2 + (j + 1))
                if not first:
                    act.wait_ge(q["S", "dn"], i * 2 + j)
                act.activation(gth[:, :], bank[4][:, 0:FP], ACT.Copy).then_inc(q["S", "ghi"], 1)
                if (c is None or isinstance(c, int) and c + j == 0) and not first:
                    result(i - 1 + j, 1 - j, isinstance(i, int) and i <= 1 - j)

            act.wait_ge(s_stp, NP)
            act.wait_ge(s_tab, 1)
            iters = pairs_of_b(act)
            high(0, 0)
            steps(act, iters, step)

        @block.tensor
        def _(pe):
            def product(dst, pairs):
                n = len(pairs)
                for m, (ah, al, bh, bl) in enumerate(pairs):
                    pe.matmul(dst, ah, bh, start=(m == 0), stop=False)
                    pe.matmul(dst, ah, bl, start=False, stop=False)
                    mm = pe.matmul(dst, al, bh, start=False, stop=(m == n - 1))
                return mm

            def modulation(i):
                pe.wait_ge(l_wm[i % 4], 16 * (i // 4 + 1))
                if i >= 2:
                    pe.wait_ge(s_modc, i - 1)
                for k in range(KD):
                    mm = pe.matmul(bank[i % 2][:, :], silb[k], ring[i % 4][:, k, :],
                                   start=(k == 0), stop=(k == KD - 1))
                mm.then_inc(s_mod, 1)

            pe.wait_ge(s_silb, KD)
            for i in range(3):
                modulation(i)
            pe.wait_ge(s_modc, 2)
            for j in range(2):
                for k in range(KD):
                    mm = pe.transpose(bank[4 + j][:, k * P:(k + 1) * P], mods[:, j, k * P:(k + 1) * P], ident)
            mm.then_inc(s_colT, 1)
            modulation(3)
            pe.wait_ge(s_cols, 1)
            pe.wait_ge(l_attn, 48)
            for n in range(KN):
                for k in range(KD):
                    mm = pe.matmul(bank[6][:, n:n + 1], btr[:, k, n * P:(n + 1) * P],
                                   cols[:, 0, k:k + 1], start=(k == 0), stop=(k == KD - 1))
            mm.then_inc(s_bsaT, 1)

            def transposes(dst, src):
                for k in range(KD):
                    mm = pe.transpose(dst[:, k * P:(k + 1) * P], src[:, k * P:(k + 1) * P], ident)
                return mm

            def up(sec, i, j, off, there=None):
                xh, xl = (xah, xal) if sec == "A" else (xbh, xbl)
                pe.wait_ge(q[sec, "xlo"], i * 2 + (j + 1))
                for m in range(KD):
                    a = slice(m * P, (m + 1) * P)
                    if there and m % (KD // 2) == 0:
                        pe.wait_ge(w_ready, there[m // (KD // 2)])
                    for h in range(2):
                        w = off + (m * UP + h * F)
                        wh, wl = whi[:, bass.ds(w, F)], wlo[:, bass.ds(w, F)]
                        dst = bank[2 + h][:, 0:F]
                        pe.matmul(dst, xh[:, j, a], wh, start=(m == 0), stop=False)
                        pe.matmul(dst, xh[:, j, a], wl, start=False, stop=False)
                        mm = pe.matmul(dst, xl[:, j, a], wh, start=False, stop=(m == KD - 1))
                mm.then_inc(q[sec, "up"], 1)

            def down(sec, i, j, off, to, there=None):
                pe.wait_ge(q[sec, "glo"], i * 2 + (j + 1))
                if there:
                    pe.wait_ge(w_ready, there)
                for m in range(KF):
                    a = slice(m * P, (m + 1) * P)
                    w = off + (WDN + m * D)
                    wh, wl = whi[:, bass.ds(w, D)], wlo[:, bass.ds(w, D)]
                    dst = bank[to + j][:, :]
                    pe.matmul(dst, gth[:, a], wh, start=(m == 0), stop=False)
                    pe.matmul(dst, gth[:, a], wl, start=False, stop=False)
                    mm = pe.matmul(dst, gtl[:, a], wh, start=False, stop=(m == KF - 1))
                mm.then_inc(q[sec, "dn"], 1)

            def turn_g(dst):
                for m in range(KF):
                    mm = pe.transpose(dst[:, m * P:(m + 1) * P], gbuf[:, m * P:(m + 1) * P], ident)
                return mm

            def body(it, lo, hi):
                if live(1, lo, hi):
                    p = it - 1
                    pe.wait_ge(s_t, p * 2 + 2)
                    if lo > 1:
                        pe.wait_ge(s_tlo, p * 2)
                    if lo > 3:
                        pe.wait_ge(q["A", "g"], (it - 4) * 2 + 2)
                    for j in range(2):
                        mm = transposes(bank[2 + j], tbuf[:, j, :])
                    mm.then_inc(s_tT, 1)
                if live(3, lo, hi):
                    p = it - 3
                    pe.wait_ge(s_h2, p * 2 + 2)
                    if lo > 3:
                        pe.wait_ge(q["A", "glo"], p * 2)
                    for j in range(2):
                        mm = transposes(bank[4 + j], h2[:, j, :])
                    mm.then_inc(s_h2T, 1)
                if live(2, lo, hi):
                    p = it - 2
                    pe.wait_ge(s_slo, p + 1)
                    if lo > 2:
                        pe.wait_ge(s_x1, p * 2)
                    if lo == 3:
                        pe.wait_ge(s_modc, 6)
                    if lo > 3:
                        pe.wait_ge(q["A", "y"], (it - 4) * 2 + 1)
                    for j in range(2):
                        t = slice(j * P, (j + 1) * P)
                        mm = product(bank[j][:, :], [(shi[:, n, t], slo[:, n, t], chi[:, n, :], clo[:, n, :])
                                                     for n in range(KN)])
                    mm.then_inc(s_at, 1)
                def last_tile():
                    if lo > 4:
                        pe.wait_ge(q["A", "y"], (it - 4) * 2)
                    down("A", it - 4, 1, 0, 0)

                if is_last(lo):
                    last_tile()
                if live(3, lo, hi):
                    p = it - 3
                    pe.wait_ge(s_xtf, p * 2 + 2)
                    if lo > 3:
                        pe.wait_ge(s_sc, p)
                        pe.wait_ge(s_rt, (it - 4) * KR + 15)
                    for j in range(2):
                        for k in range(KD):
                            mm = pe.matmul(bank[7][:, j * E:(j + 1) * E], xtf[:, j, k * P:(k + 1) * P],
                                           gw[:, k, :], start=(k == 0), stop=(k == KD - 1))
                    mm.then_inc(s_gate, 1)
                    if lo == hi == 3:
                        pe.wait_ge(w_ready, NW)
                if live(3, lo, hi):
                    if live(1, lo, hi):
                        pe.wait_ge(s_tlo, (it - 1) * 2 + 2)
                    if lo > 3:
                        pe.wait_ge(q["A", "g"], (it - 3) * 2)
                    up("A", it - 3, 0, 0)
                if live(2, lo, hi):
                    pe.wait_ge(s_x1, (it - 2) * 2 + 2)
                if live(4, lo, hi) and not is_last(lo):
                    last_tile()
                def ranks():
                    pe.wait_ge(s_rt, (it - 3) * KR + 13)
                    at_, all_ = 2 * E, 4 * E
                    pe.matmul(bank[7][:, at_:at_ + 2 * E], tri_b[:, :], mask[:, :, :], start=True, stop=False)
                    pe.matmul(bank[7][:, at_ + E:at_ + 2 * E], ones_b[:, :], mask[:, 0, :], start=False, stop=True)
                    pe.matmul(bank[7][:, all_:all_ + E], ones_b[:, :], mask[:, 0, :], start=True, stop=False)
                    pe.matmul(bank[7][:, all_:all_ + E], ones_b[:, :], mask[:, 1, :],
                              start=False, stop=True).then_inc(s_rank, 1)

                if is_last(lo):
                    ranks()
                if live(3, lo, hi):
                    pe.wait_ge(s_xtf, (it - 3) * 2 + 2)
                    pe.wait_ge(q["A", "g"], (it - 3) * 2 + 1)
                    turn_g(bank[4]).then_inc(q["A", "gt"], 1)
                if live(1, lo, hi):
                    p = it - 1
                    pe.wait_ge(s_thi, p * 2 + 2)
                    pe.wait_ge(s_tlo, p * 2 + 2)
                    if lo > 1:
                        pe.wait_ge(s_tanh, p * 2)
                    for n in range(KN):
                        t = slice(n * P, (n + 1) * P)
                        mm = product(bank[6][:, n * 2 * P:(n + 1) * 2 * P],
                                     [(bhi[:, k, t], blo[:, k, t], thi[:, k, :], tlo[:, k, :]) for k in range(KD)])
                    mm.then_inc(s_stp, 1)
                if live(3, lo, hi):
                    up("A", it - 3, 1, 0)
                    if not is_last(lo):
                        ranks()
                if live(3, lo, hi):
                    p = it - 3
                    if lo > 3:
                        pe.wait_ge(q["A", "y"], (it - 4) * 2 + 1)
                    down("A", p, 0, 0, 0)
                    pe.wait_ge(q["A", "g"], p * 2 + 2)
                    turn_g(bank[5]).then_inc(q["A", "gt"], 1)

            pe.wait_ge(s_fold, 1)
            body(1, 1, 1)
            modulation(4)
            pe.wait_ge(s_foldc, 1)
            pe.wait_ge(s_modc, 5)
            pe.wait_ge(l_gate, 32)
            body(2, 2, 2)
            pe.wait_ge(s_x1, 2)
            modulation(5)
            iterations(pe, body, 3)

            def turn(i, j):
                pe.wait_ge(q["S", "xin"][j], i * 16 + 16)
                transposes(bank[j], xin[:, j, :]).then_inc(q["S", "xt"], 1)

            off_b = [pe.alloc_register(f"off_b{j}") for j in range(2)]
            need_up = [pe.alloc_register(f"need_up{k}") for k in range(2)]
            need_dn = [pe.alloc_register(f"need_dn{j}") for j in range(2)]

            def look_up(n, j):
                pe.reg_mov(off_b[j], pe.value_load(ti[0:1, bass.ds(n + TB_OFF, 1)], min_val=0, max_val=WSZ))
                need = pe.value_load(ti[0:1, bass.ds(n + TB_NEED, 1)], min_val=NW, max_val=NW * (E + 1))
                for k in range(2):
                    pe.reg_mov(need_up[k], need + (k + 1))
                pe.reg_mov(need_dn[j], need + NW)

            def step(i, j, c, end):
                first, last = isinstance(i, int) and end, not isinstance(i, int) and end
                off = pe.snap(off_b[j], min_val=0, max_val=WSZ)
                if not last:
                    if not first:
                        pe.wait_ge(q["S", "xlo"], i * 2 + j)
                    turn(i + j, 1 - j)
                if not first:
                    pe.wait_ge(q["S", "g"], i * 2 + j)
                up("S", i, j, off, need_up)
                if not first:
                    off = pe.snap(off_b[1 - j], min_val=0, max_val=WSZ)
                    if c is None or isinstance(c, int) and 2 * c + j <= 2:
                        if not isinstance(i, int) or i * 2 + j > 2:
                            pe.wait_ge(q["S", "y"], i * 2 + (j - 2))
                    else:
                        pe.wait_ge(q["C", "y"], c * 2 + (j - 2))
                    down("S", i - 1 + j, 1 - j, off, 5, need_dn[1 - j])
                if c is None:
                    look_up(i * 2 + (j + 1), 1 - j)
                elif isinstance(c, int) and c + j == 0:
                    pe.reg_mov(off_b[1], off_b[0])
                    pe.reg_mov(need_dn[1], need_dn[0])
                pe.wait_ge(q["S", "g"], i * 2 + (j + 1))
                turn_g(bank[4]).then_inc(q["S", "gt"], 1)

            pe.wait_ge(s_tab, 1)
            iters = pairs_of_b(pe)
            pe.wait_ge(q["A", "y"], NT)
            pe.wait_ge(q["A", "glo"], NT)
            pe.wait_ge(s_tlo, NT)
            pe.wait_ge(s_tanh, NT)
            turn(0, 0)
            look_up(0, 0)
            steps(pe, iters, step)
            pe.wait_ge(q["C", "y"], NT - 2)
            down("S", iters + (NP - 1), 1, pe.snap(off_b[1], min_val=0, max_val=WSZ), 5)

        @block.vector
        def _(dve):
            count = [0]

            def link(ins, wait=True):
                count[0] += 1
                ins.then_inc(chain, 1)
                if wait:
                    dve.wait_ge(chain, count[0])

            dve.wait_ge(l_small, 32)
            link(dve.tensor_copy(tri_b[:, :], const("tri")))
            link(dve.tensor_copy(ones_b[:, :], const("ones")))
            dve.wait_ge(s_sil, 1)
            for k in range(KD):
                dve.tensor_scalar(silb[k], const("ones"), sil[:, k:k + 1], None, ALU.mult).then_inc(s_silb, 1)

            def guard(m, t, done):
                g, t1, t2 = mods[:, m, :], t[:, 0, :], t[:, 1, :]
                link(dve.tensor_scalar(t1, g, 0.0, 2.0, ALU.is_ge, ALU.mult))
                link(dve.scalar_tensor_tensor(t2, g, -1.0, g, ALU.mult, ALU.max))
                link(dve.tensor_scalar(t2, t2, 0.25, None, ALU.max))
                dve.scalar_tensor_tensor(g, t1, -1.0, t2, ALU.add, ALU.mult).then_inc(done, 1)

            io, io8 = (const(n).rearrange("p (t e) -> p t e", e=E) for n in ("io", "io8"))

            def product_a(p, j, lo):
                n = p * 2 + (j + 1)
                dve.wait_ge(q["A", "silu"], n)
                if lo > 3 or j:
                    dve.wait_ge(q["A", "gt"], p * 2 + j)
                dve.tensor_tensor(gbuf[:, 0:F], s1[:, :], bank[3][:, 0:F], ALU.mult).then_inc(q["A", "g"], 1)

            def low_a(p, j, lo):
                dve.wait_ge(q["A", "ghi"], p * 2 + (j + 1))
                dve.tensor_tensor(gtl[:, :], bank[4 + j][:, 0:FP], gth[:, :].bitcast(F32),
                                  ALU.subtract).then_inc(q["A", "glo"], 1)

            def finish_a(p, j, lo):
                dve.wait_ge(q["A", "dn"], p * 2 + (j + 1))
                if lo > 3 or j:
                    dve.wait_ge(s_fa, p * 2 + j)
                dve.tensor_tensor(fbuf, bank[j][:, :], mods[:, 5, :], ALU.mult).then_inc(q["A", "y"], 1)

            def route(it, lo, hi, *which):
                if not live(3, lo, hi):
                    return
                p = it - 3
                pair = bass.ds(p * 2, 2)

                def of_both(t):
                    return t[:, :].unsqueeze(2).to_broadcast([P, 2, E])

                for n in which:
                    if n == 0:
                        dve.wait_ge(s_sc, p + 1)
                        ins = dve.tensor_tensor(sel[:, :, :], sc[:, pair, :],
                                                rbias[:, :].unsqueeze(1).to_broadcast([P, 2, E]), ALU.add)
                    else:
                        dve.wait_ge(s_rt, p * KR + n)
                    if n in (1, 7):
                        ins = dve.tensor_reduce(rm[:, :], sel[:, :, :], AX.X, ALU.max)
                    if n in (2, 8):
                        ins = dve.tensor_tensor(ra[:, :, :], sel[:, :, :], of_both(rm), ALU.is_equal)
                    if n in (3, 9):
                        ins = dve.scalar_tensor_tensor(rc[:, :, :], ra[:, :, :], -float(E), io8, ALU.mult, ALU.add)
                    if n in (4, 10):
                        ins = dve.tensor_reduce(ri[:, :], rc[:, :, :], AX.X, ALU.min)
                    if n in (5, 11):
                        ins = dve.tensor_tensor(oh[n // 11][:, pair, :], io, of_both(ri), ALU.is_equal)
                    if n == 6:
                        ins = dve.scalar_tensor_tensor(sel[:, :, :], oh[0][:, pair, :], -BIG, sel[:, :, :],
                                                       ALU.mult, ALU.add)
                    if n == 12:
                        ins = dve.tensor_tensor(mask[:, :, :], oh[0][:, pair, :], oh[1][:, pair, :], ALU.add)
                    if n == 13:
                        dve.wait_ge(s_rank, p + 1)
                        ins = dve.tensor_tensor(rc[:, :, :], bank[7][:, 2 * E:4 * E].rearrange("p (t e) -> p t e", e=E),
                                                rbase[:, :].unsqueeze(1).to_broadcast([P, 2, E]), ALU.add)
                    if n == 14:
                        ins = dve.tensor_tensor(rbase[:, :], bank[7][:, 4 * E:5 * E], rbase[:, :], ALU.add)
                    if n in (15, 17):
                        ins = dve.tensor_tensor(ra[:, :, :], rc[:, :, :], oh[(n - 15) // 2][:, pair, :], ALU.mult)
                    if n in (16, 18):
                        ins = dve.tensor_reduce(pos[:, pair, (n - 16) // 2], ra[:, :, :], AX.X, ALU.add)
                    if n == 19:
                        if lo > 3 and not is_last(lo):
                            dve.wait_ge(s_scat, p * 64)
                        rows_of_pair = idx4[is_last(lo)][:, :].rearrange("p (t k) -> p t k", k=2)
                        ins = dve.tensor_scalar(rows_of_pair, pos[:, pair, :], 0.0, None, ALU.add)
                    ins.then_inc(s_rt, 1)

            r0 = slice(0, 1)
            S, J = SMAX, E + 2
            one = const("ones")[r0, 0:E]
            tl0 = tl[r0, :]
            total, last_n = cum[r0, E - 1:E], ordn[:, E - 1:E]
            steps_c = const("steps")[r0, :]

            def over(v, n):
                return v[r0, :].unsqueeze(1).to_broadcast([1, n, E])

            def per(c, n):
                return c.unsqueeze(2).to_broadcast([1, n, E])

            ge = big3[r0, 0:S * E].rearrange("o (s e) -> o s e", e=E)
            state = st[:, :, :].rearrange("p a b -> p (a b)")
            rows = state[r0, 0:S * E].rearrange("o (s e) -> o s e", e=E)
            nums = xtf[r0, 0, 0:S * E].rearrange("o (s e) -> o s e", e=E)
            done, used = (state[r0, S * E + n * J * E:S * E + (n + 1) * J * E].rearrange("o (s e) -> o s e", e=E)
                          for n in range(2))

            def table_rows():
                dve.wait_ge(s_rt, NP * KR)
                link(dve.tensor_tensor(nE[:, :], rbase[:, :], const("eoff"), ALU.subtract))
                b3 = big3[:, 0:E * NT].rearrange("p (e t) -> p e t", e=E)
                link(dve.tensor_tensor(b3, nE[:, :].unsqueeze(2).to_broadcast([P, E, NT]),
                                       const("thr").unsqueeze(1).to_broadcast([P, E, NT]), ALU.is_gt), False)
                dve.tensor_copy(ti[:, TB_N:TB_N + E], nE[r0, :]).then_inc(s_cnt, 1)
                dve.wait_ge(chain, count[0])
                link(dve.tensor_reduce(tl[:, :], b3, AX.X, ALU.add))
                link(dve.tensor_scalar(ne[:, :], tl0, 1.0, None, ALU.min), False)
                link(dve.tensor_tensor_scan(cum[:, :], const("ones")[:, 0:E], tl[:, :], 0.0, ALU.mult, ALU.add), False)
                link(dve.tensor_scalar(rmt[:, :], tl0, -float(P), float(R), ALU.mult, ALU.add))
                link(dve.tensor_copy(ne[:, 0:1], one[:, 0:1]), False)
                link(dve.tensor_tensor(ge, per(steps_c, S), over(cum, S), ALU.is_ge))
                link(dve.tensor_tensor_scan(ordn[:, :], one, ne[:, :], 0.0, ALU.mult, ALU.add), False)
                link(dve.tensor_tensor(rows, ge, over(rmt, S), ALU.mult), False)
                link(dve.tensor_tensor(nums, ge, over(ne, S), ALU.mult))
                link(dve.tensor_reduce(tr[:, :], rows, AX.X, ALU.add), False)
                link(dve.tensor_reduce(tq[:, 0:S], nums, AX.X, ALU.add), False)
                link(dve.tensor_copy(tq[:, S:S + 1], last_n))
                dve.scalar_tensor_tensor(ti[:, TB_ROW:TB_ROW + S], steps_c, float(P), tr[:, :],
                                         ALU.mult, ALU.add).then_inc(s_row, 1)

            def table_rest():
                link(dve.tensor_scalar(tqi[:, :], tq[:, :], 1.0, None, ALU.add), False)
                link(dve.tensor_scalar(ti[:, TB_NEED:TB_NEED + S], tq[:, 0:S], float(NW), float(NW),
                                       ALU.mult, ALU.add), False)
                link(dve.tensor_scalar(ti[:, TB_NEED + S:TB_NEED + S + 1], last_n, float(NW), float(NW),
                                       ALU.mult, ALU.add), False)
                link(dve.tensor_scalar(ev[:, :], const("even")[r0, :], total, None, ALU.is_lt))
                link(dve.tensor_scalar(tqi[:, :], tqi[:, :], 1, None, ALU.bitwise_and), False)
                link(dve.tensor_reduce(tr[:, 0:1], ev[:, :], AX.X, ALU.add), False)
                link(dve.tensor_tensor(done, over(ordn, J), per(const("jseq")[r0, :], J), ALU.is_lt), False)
                link(dve.tensor_tensor(used, over(ordn, J), per(const("jseq0")[r0, :], J), ALU.is_le))
                link(dve.tensor_scalar(ti[:, TB_OFF:TB_OFF + S + 1], tqi[:, :], float(WSZ), None, ALU.mult), False)
                link(dve.tensor_scalar(ti[:, TB_ITERS:TB_ITERS + 1], tr[:, 0:1], -2.0, None, ALU.add), False)
                link(dve.tensor_scalar(ti[:, TB_JEND:TB_JEND + 1], last_n, 2.0, None, ALU.add), False)
                link(dve.tensor_tensor(used, used, over(tl, J), ALU.mult))
                link(dve.tensor_reduce(tr[:, 1:1 + J], done, AX.X, ALU.add), False)
                link(dve.tensor_reduce(tr[:, 1 + J:1 + 2 * J], used, AX.X, ALU.add))
                dve.tensor_copy(ti[:, TB_ORDER:TB_ORDER + J], tr[:, 1:1 + J])
                dve.tensor_scalar(ti[:, TB_FIN:TB_FIN + J], tr[:, 1 + J:1 + 2 * J], 1.0, None,
                                  ALU.max).then_inc(s_tab, 1)

            def first_weights(k):
                a, b = PIECES[k]
                dve.wait_ge(s_w0, k + 1)
                dve.tensor_tensor(wlo[:, a:b], raw[:, a:b], whi[:, a:b].bitcast(F32),
                                  ALU.subtract).then_inc(w_ready, 1)

            def body(it, lo, hi):
                def between(*which):
                    if not is_last(lo):
                        route(it, lo, hi, *which)

                if live(1, lo, hi):
                    p = it - 1
                    dve.wait_ge(s_thi, p * 2 + 2)
                    if lo > 1:
                        dve.wait_ge(s_stp, p)
                    for j in range(2):
                        t = slice(j * P, (j + 1) * P)
                        dve.tensor_tensor(tlo[:, :, t], bank[2 + j][:, :].rearrange("p (k m) -> p k m", k=KD),
                                          thi[:, :, t].bitcast(F32), ALU.subtract).then_inc(s_tlo, 1)
                if live(3, lo, hi):
                    p = it - 3
                    for j in range(2):
                        dve.wait_ge(s_xtf, p * 2 + (j + 1))
                        dve.tensor_tensor(xal[:, j, :], bank[4 + j][:, :], xah[:, j, :].bitcast(F32),
                                          ALU.subtract).then_inc(q["A", "xlo"], 1)
                if live(2, lo, hi):
                    p = it - 2
                    dve.wait_ge(s_at, p + 1)
                    dve.wait_ge(s_xd, p + 1)
                    for j in range(2):
                        xt = x_all[:, bass.ds(p * 2 + j, 1), :].rearrange("p a d -> p (a d)")
                        dve.tensor_tensor(xt, bank[j][:, :], xt, ALU.add).then_inc(s_x1, 1)
                if live(0, lo, hi):
                    if lo < 4:
                        dve.wait_ge(l_x[lo // 2], 16)
                    for j in range(2):
                        xt = x_all[:, bass.ds(it * 2 + j, 1), :].rearrange("p a d -> p (a d)")
                        dve.bn_stats(bn1[:, j, :], xt).then_inc(s_bn1, 1)
                if live(2, lo, hi):
                    p = it - 2
                    done = value(dve, p * 2 + 2)
                    dve.wait_ge(l_small, 32)
                    dve.wait_ge(s_x1, done)
                    for j in range(2):
                        xt = x_all[:, bass.ds(p * 2 + j, 1), :].rearrange("p a d -> p (a d)")
                        dve.bn_stats(bn2[:, j, :], xt).then_inc(s_bn2, 1)
                if live(0, lo, hi):
                    done = value(dve, it * 2 + 2)
                    dve.wait_ge(l_small, 32)
                    dve.wait_ge(s_bn1, done)
                    for j in range(2):
                        dve.bn_aggr(mv1[:, j, :], bn1[:, j, :]).then_inc(s_st1, 1)
                if live(2, lo, hi):
                    done = value(dve, (it - 2) * 2 + 2)
                    dve.wait_ge(l_small, 32)
                    dve.wait_ge(s_bn2, done)
                    for j in range(2):
                        dve.bn_aggr(mv2[:, j, :], bn2[:, j, :]).then_inc(s_st2, 1)
                if is_last(lo):
                    route(it, lo, hi, *range(13))
                between(0)
                if live(3, lo, hi):
                    product_a(it - 3, 0, lo)
                between(1)
                if live(2, lo, hi):
                    p = it - 2
                    dve.wait_ge(s_st2, p * 2 + 2)
                    if lo > 2:
                        dve.wait_ge(s_h2T, p)
                        dve.wait_ge(s_nat, p * 16)
                    for j in range(2):
                        xt = x_all[:, bass.ds(p * 2 + j, 1), :].rearrange("p a d -> p (a d)")
                        dve.scalar_tensor_tensor(h2[:, j, :], xt, mv2[:, j, 0:1], mods[:, 4, :],
                                                 ALU.subtract, ALU.mult).then_inc(s_u, 1)
                        between(2 + j)
                else:
                    between(2, 3)
                if live(4, lo, hi):
                    finish_a(it - 4, 1, lo)
                between(4)
                if live(2, lo, hi):
                    p = it - 2
                    dve.wait_ge(s_rs2, p + 1)
                    dve.wait_ge(s_u, p * 2 + 2)
                    for j in range(2):
                        dve.scalar_tensor_tensor(h2[:, j, :], h2[:, j, :], rs2[:, j:j + 1], mods[:, 3, :],
                                                 ALU.mult, ALU.add).then_inc(s_h2, 1)
                        between(5 + j)
                else:
                    between(5, 6)
                if live(3, lo, hi) and not is_last(lo):
                    low_a(it - 3, 0, lo)
                between(7, 8)
                if live(0, lo, hi):
                    dve.wait_ge(s_rs1, it + 1)
                    if lo > 0:
                        dve.wait_ge(s_tT, it)
                        dve.wait_ge(s_xa, it * 2)
                    for j in range(2):
                        xt = x_all[:, bass.ds(it * 2 + j, 1), :].rearrange("p a d -> p (a d)")
                        dve.tensor_scalar(tbuf[:, j, :], xt, mv1[:, j, 0:1], rs1[:, j:j + 1],
                                          ALU.subtract, ALU.mult).then_inc(s_t, 1)
                        between(9 + 2 * j, 10 + 2 * j)
                else:
                    between(9, 10, 11, 12)
                if lo == 1:
                    first_weights(0)
                    first_weights(1)
                if live(1, lo, hi):
                    p = it - 1
                    dve.wait_ge(s_shi, p + 1)
                    dve.tensor_tensor(slo[:, :, :], st[:, :, :], shi[:, :, :].bitcast(F32),
                                      ALU.subtract).then_inc(s_slo, 1)
                if is_last(lo):
                    route(it, lo, hi, *range(13, KR))
                    low_a(it - 3, 0, lo)
                    table_rows()
                if live(3, lo, hi):
                    product_a(it - 3, 1, lo)
                between(13, 14, 15)
                if live(3, lo, hi):
                    finish_a(it - 3, 0, lo)
                between(16)
                if live(3, lo, hi):
                    low_a(it - 3, 1, lo)
                between(17, 18, 19)
                if is_last(lo):
                    table_rest()

            body(0, 0, 0)
            link(dve.tensor_copy(rbase[:, :], const("eoff")))
            link(dve.tensor_copy(ti[:, TB_PAR:TB_PAR + E + 4], const("par")[0:1, :]))
            dve.wait_ge(s_colT, 1)
            for j in range(2):
                cv = bank[4 + j][:, :].rearrange("p (k m) -> p k m", k=KD)[:, :, 0]
                ins = dve.tensor_copy(cols[:, j, :], cv)
                ins.then_inc(s_cols, 1) if j == 0 else link(ins)
            dve.wait_ge(l_attn, 48)
            for k in range(KD):
                dve.tensor_scalar(bhi[:, k, :], btr[:, k, :], cols[:, 1, k:k + 1], None, ALU.mult).then_inc(s_bhi, 1)
            for k in range(KD):
                dve.wait_ge(s_bhi, k + 1)
                dve.scalar_tensor_tensor(blo[:, k, :], btr[:, k, :], cols[:, 1, k:k + 1],
                                         bhi[:, k, :].bitcast(F32), ALU.mult, ALU.subtract)
            dve.wait_ge(s_modc, 3)
            guard(2, tmpa, s_ga)
            dve.wait_ge(s_bsaT, 1)
            dve.tensor_copy(bsa[:, :], bank[6][:, 0:KN]).then_inc(s_fold, 1)
            dve.wait_ge(s_fold, 1)
            dve.wait_ge(s_cga, KN)
            link(dve.tensor_copy(chi[:, :, :], cga[:, :, :]))
            dve.tensor_tensor(clo[:, :, :], cga[:, :, :], chi[:, :, :].bitcast(F32), ALU.subtract).then_inc(s_foldc, 1)
            body(1, 1, 1)
            first_weights(2)
            dve.wait_ge(s_foldc, 1)
            dve.wait_ge(l_gate, 32)
            dve.wait_ge(s_modc, 5)

            body(2, 2, 2)
            dve.wait_ge(s_modc, 6)
            guard(5, xtf, s_gb)
            dve.wait_ge(s_gb, 1)
            link(dve.memset(gbuf[:, F:FP], 0.0))
            body(3, 3, 3)
            for g in range(2, 4):
                dve.wait_ge(l_x[g], 16)
            body(4, 4, 4)
            with dve.Fori(5, NP) as it:
                body(it, 5, NP - 1)
            for it in range(NP, NP + 4):
                body(it, it, it)

            def routed():
                ty = state[:, 0:NT * E].rearrange("p (t e) -> p t e", e=E)
                yp = state[:, NT * E:NT * E + NT]
                link(dve.tensor_tensor(base[:, :], cum[:, :], tl[:, :], ALU.subtract))
                link(dve.scalar_tensor_tensor(base[:, :], base[:, :], float(P), const("eoff"),
                                              ALU.mult, ALU.subtract))
                for k in range(2):
                    link(dve.tensor_tensor(ty, oh[k][:, :, :], sc[:, :, :], ALU.mult))
                    link(dve.tensor_reduce(sw[:, k, :], ty, AX.X, ALU.add))
                    link(dve.tensor_tensor(ty, oh[k][:, :, :], base[:, :].unsqueeze(1).to_broadcast([P, NT, E]),
                                           ALU.mult))
                    link(dve.tensor_reduce(yp, ty, AX.X, ALU.add))
                    link(dve.tensor_tensor(pos[:, :, k], pos[:, :, k], yp, ALU.add))
                link(dve.tensor_tensor(den[:, :], sw[:, 0, :], sw[:, 1, :], ALU.add))
                link(dve.tensor_scalar(den[:, :], den[:, :], 1e-12, None, ALU.max))
                link(dve.reciprocal(den[:, :], den[:, :]))
                for k in range(2):
                    link(dve.tensor_tensor(wts[:, :, k], sw[:, k, :], den[:, :], ALU.mult))

            def lows(i, j):
                dve.wait_ge(q["S", "xhi"], i * 2 + (j + 1))
                dve.tensor_tensor(xbl[:, j, :], bank[j][:, :], xbh[:, j, :].bitcast(F32),
                                  ALU.subtract).then_inc(q["S", "xlo"], 1)

            def offsets(c, j, first):
                if not first:
                    dve.wait_ge(s_gath[j], c * 32)
                for k in range(2):
                    dve.tensor_copy(idx[j][k][:, :], pos[:, bass.ds(c * 2 + j, 1), k]).then_inc(q["C", "idx"], 1)

            def finish(i, c, j):
                dve.wait_ge(q["S", "dn"], i * 2 + (j + 1))
                xt = x_all[:, bass.ds(c * 2 + j, 1), :].rearrange("p a d -> p (a d)")
                y, n = ybuf[:, j, :], c * 2 + (j + 1)
                dve.wait_ge(s_gath[j], c * 32 + 32)
                if isinstance(c, int) and c == 0:
                    dve.wait_ge(q["S", "ydma"][j], iters * 16)
                else:
                    dve.wait_ge(q["C", "ydma"][j], c * 16)
                w = [wts[:, bass.ds(c * 2 + j, 1), k] for k in range(2)]
                dve.scalar_tensor_tensor(y, tbuf[:, j, :], w[0], bank[5 + j][:, :],
                                         ALU.mult, ALU.add).then_inc(q["C", "y"], 1)
                dve.wait_ge(q["C", "y"], n)
                dve.scalar_tensor_tensor(y, xtf[:, j, :], w[1], y, ALU.mult, ALU.add).then_inc(s_c2, 1)
                dve.wait_ge(s_c2, n)
                dve.tensor_tensor(y, y, mods[:, 5, :], ALU.mult).then_inc(s_c3, 1)
                dve.wait_ge(s_c3, n)
                dve.tensor_tensor(y, y, xt, ALU.add).then_inc(s_c4, 1)

            def step(i, j, c, end):
                first, last = isinstance(i, int) and end, not isinstance(i, int) and end
                if not last:
                    if not first:
                        dve.wait_ge(q["S", "up"], i * 2 + j)
                    lows(i + j, 1 - j)
                dve.wait_ge(q["S", "silu"], i * 2 + (j + 1))
                dve.wait_ge(q["S", "up"], i * 2 + (j + 1))
                if not first:
                    dve.wait_ge(q["S", "gt"], i * 2 + j)
                dve.tensor_tensor(gbuf[:, 0:F], s1[:, :], bank[3][:, 0:F], ALU.mult).then_inc(q["S", "g"], 1)
                dve.wait_ge(q["S", "ghi"], i * 2 + (j + 1))
                if not first:
                    dve.wait_ge(q["S", "dn"], i * 2 + j)
                dve.tensor_tensor(gtl[:, :], bank[4][:, 0:FP], gth[:, :].bitcast(F32),
                                  ALU.subtract).then_inc(q["S", "glo"], 1)
                if c is not None and not (isinstance(c, int) and c + j == 0):
                    finish(i - 1 + j, c - 1 + j, 1 - j)
                    if not last:
                        offsets(c + j, 1 - j, False)

            dve.wait_ge(s_stp, NP)
            dve.wait_ge(s_tab, 1)
            iters = pairs_of_b(dve)
            lows(0, 0)
            routed()
            for j in range(2):
                offsets(0, j, True)
            dve.wait_ge(s_fa, NT)
            steps(dve, iters, step)
            finish(iters + (NP - 1), NP - 1, 1)


def kernel(L0_attn_x, L0_attn_B, L0_attn_C, L0_attn_D, L0_ffn_gate_w, L0_ffn_router_bias, L0_ffn_W1,
           L0_ffn_W3, L0_ffn_W2, L0_ffn_sw1, L0_ffn_sw3, L0_ffn_sw2, L0_c, L0_wmod):
    import numpy as np
    import concourse.bacc as bacc
    from concourse.bass_utils import run_bass_kernel_spmd

    f = np.float32

    def chunks(a):
        return a.reshape(-1, P, a.shape[1]).transpose(1, 0, 2)

    packed = np.zeros((E + 2, P, WSZ), f)

    def pack(n, w1, w3, w2):
        packed[n, :, :WDN] = np.concatenate([chunks(w1), chunks(w3)], axis=2).reshape(P, WDN)
        w2p = np.zeros((FP, D), f)
        w2p[:F] = w2
        packed[n, :, WDN:] = chunks(w2p).reshape(P, KF * D)

    W1, W3, W2 = (np.asarray(a) for a in (L0_ffn_W1, L0_ffn_W3, L0_ffn_W2))
    s1, s3, s2 = (np.asarray(a) for a in (L0_ffn_sw1, L0_ffn_sw3, L0_ffn_sw2))
    for e in range(E):
        pack(e, W1[e], W3[e], W2[e])
    for n, h in ((SHARED_A, slice(0, F)), (SHARED_B, slice(F, 2 * F))):
        pack(n, s1[h].T, s3[h].T, s2[:, h].T)

    const = np.zeros((P, CW), f)

    def put(name, v):
        const[:, COL[name][0]:COL[name][1]] = v

    put("ident", np.eye(P))
    put("tri", np.triu(np.ones((P, P)), 1))
    put("ones", 1.0)
    put("io", np.tile(np.arange(E), 2))
    put("io8", np.tile(np.arange(E) + E, 2))
    put("eoff", np.arange(E) * R)
    put("steps", np.arange(SMAX))
    put("thr", np.arange(NT) * P)
    put("even", np.arange(SMAX // 2) * 2)
    put("jseq", np.arange(E + 2) + 1)
    put("jseq0", np.arange(E + 2))
    put("par", np.arange(E + 4) % 2 * WSZ)

    arrays = {
        "x": np.asarray(L0_attn_x)[0],
        "ccol": np.asarray(L0_c).reshape(KD, P).T,
        "wmod": np.asarray(L0_wmod),
        "bt": chunks(np.asarray(L0_attn_B).T),
        "ct": chunks(np.asarray(L0_attn_C).T),
        "dvec": np.asarray(L0_attn_D)[None, :],
        "gwt": chunks(np.asarray(L0_ffn_gate_w).T),
        "rb": np.asarray(L0_ffn_router_bias)[None, :],
        "w_all": packed.reshape((E + 2) * P, WSZ),
        "consts": const,
    }
    arrays = {k: np.ascontiguousarray(a) for k, a in arrays.items()}
    nc = bacc.Bacc("TRN2", target_bir_lowering=False, num_devices=1)
    args = [nc.dram_tensor(k, a.shape, mybir.dt.from_np(a.dtype), kind="ExternalInput").ap()
            for k, a in arrays.items()]
    res = nc.dram_tensor("out", (T, D), F32, kind="ExternalOutput").ap()
    build(nc, *args, res)
    r = run_bass_kernel_spmd(nc, [arrays], core_ids=[0])
    return r.results[0]["out"].reshape(1, T, D)
```
